# Optimizing a Trainium2 kernel written in Bass

```python
import numpy as np
import jax
import jax.numpy as jnp

def _softmax(x, axis=-1):
    return jax.nn.softmax(x, axis=axis)

def _gelu(x):
    return jax.nn.gelu(x, approximate=True)

def _silu(x):
    return jax.nn.silu(x)

def _sigmoid(x):
    return jax.nn.sigmoid(x)

def _layernorm(x, axis=-1, eps=1e-05):
    m = jnp.mean(x, axis=axis, keepdims=True)
    v = jnp.var(x, axis=axis, keepdims=True)
    return (x - m) / jnp.sqrt(v + eps)

def _scatter_add(tgt, idx, src, axis=0):
    return tgt.at[idx].add(src)

def _segment_sum(src, seg, n):
    return jax.ops.segment_sum(src, seg, n)
kernel_name = 'mk_decoder_preln_d1_seqx_r2_e878f8'

def setup_inputs(seed: int=0):
    np.random.seed(seed)
    _w = jnp.asarray

    def _rec_inputs():
        import jax
        import jax.numpy as jnp
        _rk = jax.random.key(seed)
        x = -0.0003929 + 0.9999 * jax.random.normal(jax.random.fold_in(_rk, 1), (16, 224, 512), jnp.float32)
        _lenS = 224 - jax.random.randint(jax.random.fold_in(_rk, 7), (16,), 0, max(1, 224 // 4) + 1, jnp.int32)
        _lenS2 = 750 - jax.random.randint(jax.random.fold_in(_rk, 8), (16,), 0, max(1, 750 // 4) + 1, jnp.int32)
        _ctx_768P = jax.random.normal(jax.random.fold_in(_rk, 11), (16, 16, 384), jnp.float32)
        _ctx_768c = jax.random.dirichlet(jax.random.fold_in(_rk, 511), 0.3 * jnp.ones((16,), jnp.float32), (16, 750))
        _ctx_768t = jnp.einsum('bsk,bkd->bsd', _ctx_768c, _ctx_768P)
        _ctx_768t = _ctx_768t * jax.lax.rsqrt(jnp.mean(jnp.square(_ctx_768t)) + 1e-12) * 0.953939
        ctx_768 = 0.00095986 + 0.999812 * (_ctx_768t + 0.3 * jax.random.normal(jax.random.fold_in(_rk, 611), (16, 750, 384), jnp.float32))
        _validS = jnp.arange(224)[None, :] < _lenS[:, None]
        _validS2 = jnp.arange(750)[None, :] < _lenS2[:, None]
        _causal = jnp.tril(jnp.ones((224, 224), dtype=bool))
        mask_BxS2_bf1 = jnp.ones((16, 750), dtype=bool)
        return (x, ctx_768, mask_BxS2_bf1)
    x, ctx_768, mask_BxS2_bf1 = _rec_inputs()

    def _L0_attn_setup():
        import jax, jax.numpy as jnp
        import numpy as np
        B, T, D = (1, 2048, 512)
        H, KD, VD = (16, 64, 64)
        MIN_THETA, MAX_THETA = (1.0, 10000.0)

        def _sin_cos(t, d, dtype):
            half = d // 2
            p = jnp.arange(half, dtype=dtype) / (half - 1)
            thetas = MIN_THETA * (MAX_THETA / MIN_THETA) ** p
            pos = jnp.arange(t, dtype=dtype)[:, None] / thetas[None, :]
            return (jnp.sin(pos), jnp.cos(pos))

        def _rope(x, sin, cos):
            d = x.shape[-1] // 2
            x_hi, x_lo = (x[..., :d], x[..., d:])
            y_lo = x_lo * cos + x_hi * sin
            y_hi = x_hi * cos - x_lo * sin
            return jnp.concatenate([y_lo, y_hi], axis=-1)
        key = jax.random.key(seed)
        k0, k1, k2 = jax.random.split(key, 3)
        x = jax.random.normal(k0, (B, T, D), dtype=jnp.float32)
        W_in = jax.random.normal(k1, ((2 * KD + VD) * H, D), dtype=jnp.float32) * 0.02
        b_in = jnp.zeros(((2 * KD + VD) * H,), dtype=jnp.float32)
        W_out = jax.random.normal(k2, (D, H * VD), dtype=jnp.float32) * 0.02
        b_out = jnp.zeros((D,), dtype=jnp.float32)
        return {'x': x, 'W_in': W_in, 'b_in': b_in, 'W_out': W_out, 'b_out': b_out}
    _L0_attn_all = _L0_attn_setup()
    _L0_attn_in = {k: v for k, v in _L0_attn_all.items() if k in ('W_in', 'b_in', 'W_out', 'b_out')}
    del _L0_attn_all

    def _L0_xattn_setup():
        import jax, jax.numpy as jnp
        import numpy as np
        DIM = 512
        CTX_DIM = 384
        HEADS = 16
        key = jax.random.key(seed)
        ks = jax.random.split(key, 7)
        B, N, M = (4, 2048, 128)
        x = jax.random.normal(ks[0], (B, N, DIM), dtype=jnp.float32)
        context = jax.random.normal(ks[1], (B, M, CTX_DIM), dtype=jnp.float32)
        context_mask = jnp.ones((B, M), dtype=bool)
        s_d = 1.0 / np.sqrt(DIM)
        s_c = 1.0 / np.sqrt(CTX_DIM)
        Wq = jax.random.normal(ks[2], (DIM, DIM), dtype=jnp.float32) * s_d
        Wk = jax.random.normal(ks[3], (CTX_DIM, DIM), dtype=jnp.float32) * s_c
        Wv = jax.random.normal(ks[4], (CTX_DIM, DIM), dtype=jnp.float32) * s_c
        Wo = jax.random.normal(ks[5], (DIM, DIM), dtype=jnp.float32) * s_d
        return {'x': x, 'context': context, 'context_mask': context_mask, 'Wq': Wq, 'Wk': Wk, 'Wv': Wv, 'Wo': Wo}
    _L0_xattn_all = _L0_xattn_setup()
    _L0_xattn_in = {k: v for k, v in _L0_xattn_all.items() if k in ('Wq', 'Wk', 'Wv', 'Wo')}
    del _L0_xattn_all

    def _L0_ffn_setup():
        import jax, jax.numpy as jnp
        import numpy as np
        E = 8
        K = 2
        CF = 1.25
        key = jax.random.key(seed)
        kx, kr, kg, ku, kd = jax.random.split(key, 5)
        D, F = (512, 2048)
        x = jax.random.normal(kx, (4, 1024, D), dtype=jnp.float32)
        router_w = 0.02 * jax.random.normal(kr, (E, D), dtype=jnp.float32)
        wg = jax.random.normal(kg, (E, D, F), dtype=jnp.float32) / np.sqrt(D)
        wu = jax.random.normal(ku, (E, D, F), dtype=jnp.float32) / np.sqrt(D)
        wd = jax.random.normal(kd, (E, F, D), dtype=jnp.float32) / np.sqrt(F)
        return {'x': x, 'router_w': router_w, 'wg': wg, 'wu': wu, 'wd': wd}
    _L0_ffn_all = _L0_ffn_setup()
    _L0_ffn_in = {k: v for k, v in _L0_ffn_all.items() if k in ('router_w', 'wg', 'wu', 'wd')}
    del _L0_ffn_all
    return {'x': x, 'ctx_768': ctx_768, 'mask_BxS2_bf1': mask_BxS2_bf1, 'L0_attn_W_in': _L0_attn_in['W_in'], 'L0_attn_b_in': _L0_attn_in['b_in'], 'L0_attn_W_out': _L0_attn_in['W_out'], 'L0_attn_b_out': _L0_attn_in['b_out'], 'L0_xattn_Wq': _L0_xattn_in['Wq'], 'L0_xattn_Wk': _L0_xattn_in['Wk'], 'L0_xattn_Wv': _L0_xattn_in['Wv'], 'L0_xattn_Wo': _L0_xattn_in['Wo'], 'L0_ffn_router_w': _L0_ffn_in['router_w'], 'L0_ffn_wg': _L0_ffn_in['wg'], 'L0_ffn_wu': _L0_ffn_in['wu'], 'L0_ffn_wd': _L0_ffn_in['wd']}

def reference(x, ctx_768, mask_BxS2_bf1, L0_attn_W_in, L0_attn_b_in, L0_attn_W_out, L0_attn_b_out, L0_xattn_Wq, L0_xattn_Wk, L0_xattn_Wv, L0_xattn_Wo, L0_ffn_router_w, L0_ffn_wg, L0_ffn_wu, L0_ffn_wd):
    import jax
    import jax.numpy as jnp

    def _L0_attn_ref(x, W_in, b_in, W_out, b_out):
        import jax, jax.numpy as jnp
        import numpy as np
        B, T, D = (1, 2048, 512)
        H, KD, VD = (16, 64, 64)
        MIN_THETA, MAX_THETA = (1.0, 10000.0)

        def _sin_cos(t, d, dtype):
            half = d // 2
            p = jnp.arange(half, dtype=dtype) / (half - 1)
            thetas = MIN_THETA * (MAX_THETA / MIN_THETA) ** p
            pos = jnp.arange(t, dtype=dtype)[:, None] / thetas[None, :]
            return (jnp.sin(pos), jnp.cos(pos))

        def _rope(x, sin, cos):
            d = x.shape[-1] // 2
            x_hi, x_lo = (x[..., :d], x[..., d:])
            y_lo = x_lo * cos + x_hi * sin
            y_hi = x_hi * cos - x_lo * sin
            return jnp.concatenate([y_lo, y_hi], axis=-1)
        b, t, _ = x.shape
        proj = x @ W_in.T + b_in
        i1, i2 = (KD * H, 2 * KD * H)
        q = proj[..., :i1].reshape(b, t, H, KD).transpose(0, 2, 1, 3)
        k = proj[..., i1:i2].reshape(b, t, H, KD).transpose(0, 2, 1, 3)
        v = proj[..., i2:].reshape(b, t, H, VD).transpose(0, 2, 1, 3)
        sin, cos = _sin_cos(t, KD, x.dtype)
        q = _rope(q, sin, cos)
        k = _rope(k, sin, cos)
        scale = 1.0 / np.sqrt(KD)
        att = jnp.einsum('bhqd,bhkd->bhqk', q, k) * jnp.asarray(scale, x.dtype)
        mask = jnp.tril(jnp.ones((t, t), dtype=bool))
        att = jnp.where(mask[None, None], att, jnp.asarray(-jnp.inf, x.dtype))
        att = jax.nn.softmax(att, axis=-1)
        y = jnp.einsum('bhqk,bhkd->bhqd', att, v)
        y = y.transpose(0, 2, 1, 3).reshape(b, t, H * VD)
        return y @ W_out.T + b_out

    def _L0_xattn_ref(x, context, context_mask, Wq, Wk, Wv, Wo):
        import jax, jax.numpy as jnp
        import numpy as np
        DIM = 512
        CTX_DIM = 384
        HEADS = 16
        B, N, _ = x.shape
        M = context.shape[1]
        hd = DIM // HEADS
        scale = hd ** (-0.5)
        q = (x @ Wq).reshape(B, N, HEADS, hd).transpose(0, 2, 1, 3)
        k = (context @ Wk).reshape(B, M, HEADS, hd).transpose(0, 2, 1, 3)
        v = (context @ Wv).reshape(B, M, HEADS, hd).transpose(0, 2, 1, 3)
        scores = jnp.einsum('bhid,bhjd->bhij', q, k) * scale
        max_neg = -jnp.finfo(scores.dtype).max
        scores = jnp.where(context_mask[:, None, None, :], scores, max_neg)
        attn = jax.nn.softmax(scores, axis=-1)
        out = jnp.einsum('bhij,bhjd->bhid', attn, v)
        out = out.transpose(0, 2, 1, 3).reshape(B, N, DIM)
        return out @ Wo

    def _L0_ffn_ref(x, router_w, wg, wu, wd):
        import jax, jax.numpy as jnp
        import numpy as np
        E = 8
        K = 2
        CF = 1.25
        B, L, D = x.shape
        xf = x.reshape(-1, D)
        N = xf.shape[0]
        capacity = max(1, int(CF * N / E))
        logits = xf @ router_w.T
        probs = jax.nn.softmax(logits, axis=-1)
        topw, topi = jax.lax.top_k(probs, K)
        topw = topw / (topw.sum(-1, keepdims=True) + 1e-06)
        fe = topi.reshape(-1)
        fw = topw.reshape(-1)
        ft = jnp.repeat(jnp.arange(N), K)
        order = jnp.lexsort((-fw, fe))
        se, sw, st = (fe[order], fw[order], ft[order])
        counts = jax.ops.segment_sum(jnp.ones_like(se), se, num_segments=E)
        starts = jnp.cumsum(counts) - counts
        rank = jnp.arange(N * K) - starts[se]
        keep = rank < capacity
        pos = jnp.where(keep, rank, capacity)
        disp = jnp.zeros((E, capacity + 1, D), x.dtype).at[se, pos].set(xf[st])
        disp = disp[:, :capacity]
        g = jnp.einsum('ecd,edf->ecf', disp, wg)
        u = jnp.einsum('ecd,edf->ecf', disp, wu)
        eo = jnp.einsum('ecf,efd->ecd', jax.nn.silu(g) * u, wd)
        gathered = eo[se, jnp.minimum(pos, capacity - 1)]
        contrib = gathered * (sw * keep.astype(x.dtype))[:, None]
        out = jnp.zeros_like(xf).at[st].add(contrib)
        return out.reshape(B, L, D)
    x = x + _L0_attn_ref(_layernorm(x, axis=-1), L0_attn_W_in, L0_attn_b_in, L0_attn_W_out, L0_attn_b_out)
    x = x + _L0_xattn_ref(_layernorm(x, axis=-1), ctx_768, mask_BxS2_bf1, L0_xattn_Wq, L0_xattn_Wk, L0_xattn_Wv, L0_xattn_Wo)
    x = x + _L0_ffn_ref(_layernorm(x, axis=-1), L0_ffn_router_w, L0_ffn_wg, L0_ffn_wu, L0_ffn_wd)
    return x

_drawn_inputs = setup_inputs


def setup_inputs(seed=0):
    import zlib

    import numpy as np

    out = dict(_drawn_inputs(seed))
    spreads = {'L0_attn_b_in': (0.0, 0.1), 'L0_attn_b_out': (0.0, 0.1)}
    factors = {}
    for name, (base, spread) in spreads.items():
        noise = np.random.default_rng([zlib.crc32(name.encode()), seed]).standard_normal(out[name].shape)
        drawn = base * np.exp(spread * noise) if base else spread * noise
        out[name] = jnp.asarray(drawn.astype(out[name].dtype))
    for name, factor in factors.items():
        out[name] = (out[name] * factor).astype(out[name].dtype)
    return out
```

```python
import concourse.bass as bass
from concourse import mybir
from contextlib import ExitStack
import numpy as np

F32 = mybir.dt.float32
F32R = mybir.dt.float32r
I32 = mybir.dt.int32
U32 = mybir.dt.uint32
ALU = mybir.AluOpType
ACT = mybir.ActivationFunctionType
AX = mybir.AxisListType

B, T, D = 16, 224, 512
N = B * T
P = 128
HT = T // 2
KD = D // P
EPS = 1e-5

SH, SD = 16, 64
SG = SH // 4
SV = SH * SD

NEG = -3.0e38


def mm3(pe, out, lhs, rhs, first, last):
    (lh, ll), (rh, rl) = lhs, rhs
    pe.matmul(out, lh, rh, start=first, stop=False)
    pe.matmul(out, lh, rl, start=False, stop=False)
    return pe.matmul(out, ll, rh, start=False, stop=last)


def hold(e, gate, sem, value):
    e.wait_ge(sem, value)
    if not isinstance(value, int):
        e.sem_inc(gate, 1)


def layer_norm_steps(dve, gate, done, count, stats, mv, work, tiles, outs):
    n = len(tiles)
    k = 0

    def step(ins):
        nonlocal k
        k += 1
        ins.then_inc(done, 1)

    for i, t in enumerate(tiles):
        step(dve.bn_stats(stats[:, i, :], t))
    dve.wait_ge(done, count + k)
    dve.sem_inc(gate, 1)
    for i in range(n):
        step(dve.bn_aggr(mv[:, i, :], stats[:, i:i + 1, :]))
    dve.wait_ge(done, count + k)
    v, y, a, b = (work[:, j * n:(j + 1) * n] for j in range(4))
    step(dve.tensor_scalar(v, mv[:, 0:n, 1], EPS, None, ALU.add))
    dve.wait_ge(done, count + k)
    step(dve.tensor_scalar(y.bitcast(I32), v.bitcast(I32), 1, None, ALU.arith_shift_right))
    dve.wait_ge(done, count + k)
    step(dve.tensor_scalar(y.bitcast(I32), y.bitcast(I32), -1.0, float(0x5F3759DF), ALU.mult, ALU.add))
    dve.wait_ge(done, count + k)
    for _ in range(4):
        step(dve.tensor_tensor(a, y, y, ALU.mult))
        dve.wait_ge(done, count + k)
        step(dve.tensor_tensor(b, a, v, ALU.mult))
        dve.wait_ge(done, count + k)
        step(dve.tensor_scalar(a, b, -0.5, 1.5, ALU.mult, ALU.add))
        dve.wait_ge(done, count + k)
        step(dve.tensor_tensor(y, y, a, ALU.mult))
        dve.wait_ge(done, count + k)
    for i, t in enumerate(tiles):
        step(dve.tensor_scalar(outs[i], t, mv[:, i, 0:1], y[:, i:i + 1], ALU.subtract, ALU.mult))
    return k


LN_STEPS = 2 + 2 + 3 + 16 + 2


def self_attention(nc, x, w_in, b_in, w_out, b_out, cst, x1):
    with ExitStack() as outer:
        def sb(stack, name, shape, dt=F32):
            return stack.enter_context(nc.sbuf_tensor(name, shape, dt))

        def sem(name):
            return outer.enter_context(nc.semaphore(name))

        ident = sb(outer, "ident", [P, P])
        win_hi = sb(outer, "win_hi", [P, KD, 3 * SV], F32R)
        win_lo = sb(outer, "win_lo", [P, KD, 3 * SV], F32R)
        wout = sb(outer, "wout", [P, SV // P, D])
        bias = sb(outer, "bias", [P, 24])
        obias = sb(outer, "obias", [HT, D])

        with ExitStack() as c:
            nat = sb(c, "nat", [P, 4, D])
            brow = sb(c, "brow", [24, P])
            bvb = sb(c, "bvb", [P, 8, HT])
            bo = sb(c, "bo", [HT, D])
            ps = [c.enter_context(nc.psum_tensor(f"w_ps{i}", [P, 512], F32)) for i in range(4)]
            nat_loaded = [sem(f"nat_loaded{i}") for i in range(4)]
            small_loaded, w_turned, w_high, w_low, b_turned, b_spread, ob_done = (
                sem(n) for n in ("small_loaded", "w_turned", "w_high", "w_low", "b_turned", "b_spread", "ob_done"))
            wo_v = w_out.rearrange("(r p) (h k) -> r h p k", p=P, h=2)
            with nc.Block() as block:
                @block.sync
                def _(sp):
                    sp.dma_start(ident[:], cst[:, 0:P]).then_inc(small_loaded, 16)
                    sp.dma_start(brow[:], b_in.rearrange("(c p) -> c p", p=P)).then_inc(small_loaded, 16)
                    sp.dma_start(bo[:], b_out.rearrange("(o n) -> o n", o=1).to_broadcast((HT, D))).then_inc(small_loaded, 16)
                    for s in range(4):
                        sp.dma_start(nat[:, s, :], w_in[s * P:(s + 1) * P, :]).then_inc(nat_loaded[s], 16)
                    with sp.Fori(1, 6) as i:
                        for s in range(4):
                            sp.wait_ge(w_turned, 4 * i + s - 3)
                            sp.dma_start(nat[:, s, :], w_in[bass.ds(i * 512 + s * P, P), :]).then_inc(nat_loaded[s], 16)
                    for u in range(8):
                        sp.wait_ge(w_turned, 24 + u - 3)
                        sp.dma_start(nat[:, u % 4, :], wo_v[u // 2, u % 2, :, :]).then_inc(nat_loaded[u % 4], 16)

                @block.tensor
                def _(pe):
                    pe.wait_ge(small_loaded, 48)

                    def turn(u, s, round_):
                        pe.wait_ge(nat_loaded[s], 16 * round_ + 16)
                        for k in range(KD):
                            m = pe.transpose(ps[s][:, k * P:(k + 1) * P], nat[:, s, k * P:(k + 1) * P], ident[:])
                        m.then_inc(w_turned, 1)

                    for s in range(4):
                        turn(s, s, 0)
                    with pe.Fori(1, 6) as i:
                        for s in range(4):
                            pe.wait_ge(w_high, 4 * i + s - 3)
                            pe.wait_ge(w_low, 4 * i + s - 3)
                            turn(4 * i + s, s, i)
                    for u in range(24, 32):
                        pe.wait_ge(w_high, u - 3)
                        if u < 28:
                            pe.wait_ge(w_low, u - 3)
                        turn(u, u % 4, u // 4)
                    pe.wait_ge(w_high, 32)
                    pe.transpose(ps[0][:, 0:24], brow[:], ident[0:24, 0:24]).then_inc(b_turned, 1)
                    pe.wait_ge(b_spread, 2)
                    for k in range(8):
                        m = pe.matmul(ps[1][0:HT, :], bvb[:, k, :], wout[:, k, :], start=(k == 0), stop=(k == 7))
                    m.then_inc(ob_done, 1)

                @block.scalar
                def _(act):
                    with act.Fori(0, 6) as i:
                        for s in range(4):
                            act.wait_ge(w_turned, 4 * i + s + 1)
                            act.activation(win_hi[:, :, bass.ds(i * 512 + s * P, P)],
                                           ps[s][:].rearrange("p (k c) -> p k c", k=KD), ACT.Copy).then_inc(w_high, 1)
                    for u in range(8):
                        act.wait_ge(w_turned, 25 + u)
                        act.activation(wout[:, 4 * (u % 2):4 * (u % 2) + 4, (u // 2) * P:(u // 2 + 1) * P],
                                       ps[u % 4][:].rearrange("p (k c) -> p k c", k=KD), ACT.Copy).then_inc(w_high, 1)

                @block.vector
                def _(dve):
                    with dve.Fori(0, 6) as i:
                        for s in range(4):
                            dve.wait_ge(w_high, 4 * i + s + 1)
                            dve.tensor_tensor(win_lo[:, :, bass.ds(i * 512 + s * P, P)],
                                              ps[s][:].rearrange("p (k c) -> p k c", k=KD),
                                              win_hi[:, :, bass.ds(i * 512 + s * P, P)].bitcast(F32),
                                              ALU.subtract).then_inc(w_low, 1)
                    dve.wait_ge(b_turned, 1)
                    dve.tensor_copy(bias[:], ps[0][:, 0:24]).then_inc(b_spread, 1)
                    dve.wait_ge(b_spread, 1)
                    dve.tensor_copy(bvb[:], bias[:, 16:24].unsqueeze(2).to_broadcast((P, 8, HT))).then_inc(b_spread, 1)
                    dve.wait_ge(ob_done, 1)
                    dve.tensor_tensor(obias[:], ps[1][0:HT, :], bo[:], ALU.add).then_inc(b_spread, 1)

        with ExitStack() as c:
            xt = sb(c, "xt", [HT, 2, D])
            xres = sb(c, "xres", [HT, 2, D])
            osb = sb(c, "osb", [HT, 2, D])
            stats, mv, lnw = sb(c, "stats", [HT, 2, 6]), sb(c, "mv", [HT, 2, 2]), sb(c, "lnw", [HT, 8])
            xraw = sb(c, "xraw", [P, KD, T])
            xT_hi, xT_lo = sb(c, "xT_hi", [P, KD, T], F32R), sb(c, "xT_lo", [P, KD, T], F32R)
            ssin, cos = sb(c, "ssin", [P, T]), sb(c, "cos", [P, T])
            mask = sb(c, "mask", [HT, 2, T])
            v = sb(c, "v", [HT, 2, SV])
            qk = [sb(c, f"qk{i}", [P, 4, T]) for i in range(2)]
            qks = [sb(c, f"qks{i}", [P, 4, T]) for i in range(2)]
            q_hi = [sb(c, f"q_hi{i}", [P, 2, T], F32R) for i in range(2)]
            q_lo = [sb(c, f"q_lo{i}", [P, 2, T], F32R) for i in range(2)]
            k_hi = [sb(c, f"k_hi{i}", [P, 2, 2, T], F32R) for i in range(2)]
            k_lo = [sb(c, f"k_lo{i}", [P, 2, 2, T], F32R) for i in range(2)]
            sm = sb(c, "sm", [HT, 4, 3 * HT])
            mx, nm = sb(c, "mx", [HT, 4, 2]), sb(c, "nm", [HT, 4, 2])
            sums, rs = sb(c, "sums", [HT, 4, 2]), sb(c, "rs", [HT, 4, 2])
            pr = sb(c, "pr", [HT, 4, 3 * HT])
            pt = sb(c, "pt", [HT, 4, 3 * HT])
            yT = sb(c, "yT", [P, SV // P, T])
            pj = [c.enter_context(nc.psum_tensor(f"pj{i}", [P, 512], F32)) for i in range(2)]
            psS = [c.enter_context(nc.psum_tensor(f"psS{i}", [P, 512], F32)) for i in range(2)]
            psT = [c.enter_context(nc.psum_tensor(f"psT{i}", [P, 512], F32)) for i in range(2)]
            psY = [c.enter_context(nc.psum_tensor(f"psY{i}", [P, 512], F32)) for i in range(2)]

            const_loaded, zeroed, x_loaded, xres_loaded, xres_ready, stored, ln, xT_ready = (
                sem(n) for n in ("const_loaded", "zeroed", "x_loaded", "xres_loaded", "xres_ready",
                                 "stored", "ln", "xT_ready"))
            pj_full, pj_free, qk_out, turned, qk_ready, s_full, sm_ready, p_ready, recip, pn_ready = (
                sem(n) for n in ("pj_full", "pj_free", "qk_out", "turned", "qk_ready", "s_full", "sm_ready",
                                 "p_ready", "recip", "pn_ready"))
            t_full, pt_ready, y_full, y_ready, o_ready, rope, mxd = (
                sem(n) for n in ("t_full", "pt_ready", "y_full", "y_ready", "o_ready", "rope", "mxd"))
            gate = sem("gate")
            swapped = [sem(f"swapped{i}") for i in range(2)]
            SWAPS = [(0, 32), (32, 0), (64, 96), (96, 64)]
            PRE = 10
            PER = 16

            xv = x.rearrange("b (h p) d -> b p h d", p=HT)

            with nc.Block() as block:
                @block.sync
                def _(sp):
                    sp.dma_start(ssin[:], cst[:, 128:352]).then_inc(const_loaded, 16)
                    sp.dma_start(cos[:], cst[:, 352:576]).then_inc(const_loaded, 16)
                    sp.dma_start(mask[:].rearrange("p a t -> p (a t)"), cst[0:HT, 576:1024]).then_inc(const_loaded, 16)
                    sp.dma_start(xt[:], xv[0]).then_inc(x_loaded, 16)

                    def swap(t, g, b):
                        par = g % 2
                        hold(sp, gate, qk_out, t + 1)
                        if not (isinstance(t, int) and t < 2):
                            hold(sp, gate, qk_ready, t - 1)
                        for dst, src in SWAPS:
                            sp.dma_start(qks[par][dst:dst + 32, :, :], qk[par][src:src + 32, :, :]).then_inc(swapped[par], 16)

                    def steps(b, last, ahead):
                        swap(4 * b + 2, 2, b)
                        swap(4 * b + 3, 3, b)
                        if ahead:
                            hold(sp, gate, xT_ready, b + 2)
                            sp.dma_start(xt[:], xv[bass.ds(b + 2, 1)].rearrange("o p h d -> (o p) h d")).then_inc(x_loaded, 16)
                        if not last:
                            swap(4 * b + 4, 0, b + 1)
                            swap(4 * b + 5, 1, b + 1)
                        hold(sp, gate, o_ready, b + 1)
                        dst = x1.rearrange("(b h p) d -> b p h d", p=HT, h=2)
                        dst = dst[b] if isinstance(b, int) else dst[bass.ds(b, 1)].rearrange("o p h d -> (o p) h d")
                        sp.dma_start(dst, osb[:]).then_inc(stored, 16)
                        hold(sp, gate, stored, 16 * b + 16)
                        if not last:
                            src = xv[b + 1] if isinstance(b, int) else xv[bass.ds(b + 1, 1)].rearrange("o p h d -> (o p) h d")
                            sp.dma_start(xres[:], src).then_inc(xres_loaded, 16)

                    sp.dma_start(xres[:], xv[0]).then_inc(xres_loaded, 16)
                    hold(sp, gate, xT_ready, 1)
                    sp.dma_start(xt[:], xv[1]).then_inc(x_loaded, 16)
                    swap(0, 0, 0)
                    swap(1, 1, 0)
                    with sp.Fori(0, B - 2) as b:
                        steps(b, False, True)
                    steps(B - 2, False, False)
                    steps(B - 1, True, False)

                @block.tensor
                def _(pe):
                    xTk = lambda k, a=0, n=T: (xT_hi[:, k, a:a + n], xT_lo[:, k, a:a + n])

                    def unit(u):
                        if not (isinstance(u, int) and u < 2):
                            pe.wait_ge(pj_free, u - 1)

                    def turn_x(u, b):
                        pe.wait_ge(ln, LN_STEPS * b + LN_STEPS)
                        for h in range(2):
                            unit(u + h)
                            for k in range(KD):
                                m = pe.transpose(pj[h][:, k * HT:(k + 1) * HT], xt[:, h, k * P:(k + 1) * P], ident[0:HT, 0:HT])
                            m.then_inc(pj_full, 1)

                    def project_qk(u, g):
                        for s in range(2):
                            unit(u + s)
                            for i in range(2):
                                cols = s * SV + (2 * g + i) * P
                                for k in range(KD):
                                    m = mm3(pe, pj[s][:, i * T:(i + 1) * T],
                                            (win_hi[:, k, cols:cols + P], win_lo[:, k, cols:cols + P]),
                                            xTk(k), k == 0, k == KD - 1)
                            m.then_inc(pj_full, 1)

                    def project_v(u):
                        for i in range(4):
                            h, n = divmod(i, 2)
                            unit(u + i)
                            cols = 2 * SV + n * 512
                            for k in range(KD):
                                m = mm3(pe, pj[i % 2][0:HT, :], xTk(k, h * HT, HT),
                                        (win_hi[:, k, cols:cols + 512], win_lo[:, k, cols:cols + 512]),
                                        k == 0, k == KD - 1)
                            m.then_inc(pj_full, 1)

                    def project_out(u, b):
                        pe.wait_ge(y_ready, 4 * b + 4)
                        for h in range(2):
                            unit(u + h)
                            for k in range(8):
                                m = pe.matmul(pj[h][0:HT, :], yT[:, k, h * HT:(h + 1) * HT], wout[:, k, :],
                                              start=(k == 0), stop=(k == 7))
                            m.then_inc(pj_full, 1)

                    def scores(t, g, heads=range(4)):
                        par = g % 2
                        if 0 in heads:
                            pe.wait_ge(qk_ready, t + 1)
                        for j in heads:
                            n = 4 * t + j
                            if not (isinstance(n, int) and n < 2):
                                pe.wait_ge(sm_ready, n - 1)
                            i, hd = divmod(j, 2)
                            for h in range(2):
                                q = (q_hi[par][:, i, h * HT:(h + 1) * HT], q_lo[par][:, i, h * HT:(h + 1) * HT])
                                m = mm3(pe, psS[j % 2][0:HT, h * T:(h + 1) * T], q,
                                        (k_hi[par][:, i, hd, :], k_lo[par][:, i, hd, :]), True, True)
                            m.then_inc(s_full, 1)

                    def turn_p(t, j):
                        n = 4 * t + j
                        pe.wait_ge(pn_ready, n + 1)
                        if j >= 2:
                            pe.wait_ge(pt_ready, n - 1)
                        for r in range(3):
                            m = pe.transpose(psT[j % 2][0:HT, r * HT:(r + 1) * HT], pr[:, j, r * HT:(r + 1) * HT], ident[0:HT, 0:HT])
                        m.then_inc(t_full, 1)

                    def values(t, g, p):
                        if p == 0 and g >= 2:
                            pe.wait_ge(y_ready, t - 1)
                        pe.wait_ge(pt_ready, 4 * t + 2 * p + 2)
                        for r in range(2):
                            for hd in range(2):
                                cols = (4 * g + 2 * p + hd) * SD
                                m = pe.matmul(psY[g % 2][hd * SD:hd * SD + SD, p * T + r * HT:(p + 1) * T], v[:, r, cols:cols + SD],
                                              pt[:, 2 * p + hd, r * T:T + r * HT], start=(r == 0), stop=(r == 1))
                        if p == 1:
                            m.then_inc(y_full, 1)

                    def attend(t, g):
                        for j in range(4):
                            turn_p(t, j)
                            if j == 3:
                                values(t, g, 0)
                        values(t, g, 1)

                    def attend_and_score(t, g):
                        turn_p(t, 0)
                        turn_p(t, 1)
                        scores(t + 1, g + 1, range(0, 2))
                        turn_p(t, 2)
                        turn_p(t, 3)
                        values(t, g, 0)
                        scores(t + 1, g + 1, range(2, 3))
                        values(t, g, 1)
                        scores(t + 1, g + 1, range(3, 4))

                    pe.wait_ge(zeroed, 1)
                    turn_x(0, 0)
                    pe.wait_ge(xT_ready, 1)
                    project_qk(2, 0)
                    project_qk(4, 1)
                    project_v(6)
                    scores(0, 0)

                    def steps(b, last):
                        t, u = 4 * b, PRE + PER * b
                        project_qk(u, 2)
                        attend_and_score(t, 0)
                        project_qk(u + 2, 3)
                        attend(t + 1, 1)
                        scores(t + 2, 2)
                        u = u + 4
                        if not last:
                            turn_x(u, b + 1)
                            u = u + 2
                        attend(t + 2, 2)
                        if not last:
                            pe.wait_ge(xT_ready, b + 2)
                            project_qk(u, 0)
                            u = u + 2
                        scores(t + 3, 3)
                        if not last:
                            project_qk(u, 1)
                            u = u + 2
                        attend(t + 3, 3)
                        if not last:
                            project_v(u)
                            u = u + 4
                        project_out(u, b)
                        if not last:
                            scores(t + 4, 0)

                    with pe.Fori(0, B - 1) as b:
                        steps(b, False)
                    steps(B - 1, True)

                @block.scalar
                def _(act):
                    def out_x(u):
                        for h in range(2):
                            act.wait_ge(pj_full, u + h + 1)
                            act.activation(xraw[:, :, h * HT:(h + 1) * HT],
                                           pj[h][:, 0:KD * HT].rearrange("p (k c) -> p k c", k=KD), ACT.Copy).then_inc(pj_free, 1)

                    def out_qk(u, t, g):
                        par = g % 2
                        if not (isinstance(t, int) and t < 2):
                            act.wait_ge(qk_ready, t - 1)
                        for s in range(2):
                            act.wait_ge(pj_full, u + s + 1)
                            for i in range(2):
                                col = s * 8 + 2 * g + i
                                m = act.activation(qk[par][:, 2 * s + i, :], pj[s][:, i * T:(i + 1) * T], ACT.Identity,
                                                   bias=bias[:, col:col + 1])
                                if i == 1:
                                    m.then_inc(pj_free, 1)
                        act.wait_ge(pj_free, u + 2)
                        act.nop().then_inc(qk_out, 1)

                    def out_v(u):
                        for i in range(4):
                            act.wait_ge(pj_full, u + i + 1)
                            act.activation(v[:, i // 2, (i % 2) * 512:(i % 2) * 512 + 512], pj[i % 2][0:HT, :], ACT.Copy).then_inc(pj_free, 1)

                    def out_o(u, b):
                        act.wait_ge(xres_loaded, 16 * b + 16)
                        for h in range(2):
                            act.wait_ge(pj_full, u + h + 1)
                            act.activation(osb[:, h, :], pj[h][0:HT, :], ACT.Copy).then_inc(pj_free, 1)

                    def exps(t, g):
                        for j in range(4):
                            n = 4 * t + j
                            act.wait_ge(sm_ready, n + 1)
                            if not (isinstance(t, int) and t == 0):
                                act.wait_ge(t_full, n - 3)
                            act.activation(pr[:, j, 0:HT], sm[:, j, 0:HT], ACT.Exp, bias=nm[:, j, 0:1], scale=SD ** -0.5,
                                           accum_out=sums[:, j, 0:1])
                            act.activation(pr[:, j, HT:3 * HT], sm[:, j, HT:3 * HT], ACT.Exp, bias=nm[:, j, 1:2], scale=SD ** -0.5,
                                           accum_out=sums[:, j, 1:2]).then_inc(p_ready, 1)

                    def out_p(t):
                        for j in range(4):
                            n = 4 * t + j
                            act.wait_ge(t_full, n + 1)
                            act.activation(pt[:, j, :], psT[j % 2][0:HT, 0:3 * HT], ACT.Copy).then_inc(pt_ready, 1)

                    out_x(0)
                    out_qk(2, 0, 0)
                    out_qk(4, 1, 1)
                    out_v(6)
                    exps(0, 0)

                    def steps(b, last):
                        t, u = 4 * b, PRE + PER * b
                        out_qk(u, t + 2, 2)
                        out_p(t)
                        exps(t + 1, 1)
                        out_qk(u + 2, t + 3, 3)
                        out_p(t + 1)
                        exps(t + 2, 2)
                        u = u + 4
                        if not last:
                            out_x(u)
                            u = u + 2
                        out_p(t + 2)
                        if not last:
                            out_qk(u, t + 4, 0)
                            u = u + 2
                        exps(t + 3, 3)
                        if not last:
                            out_qk(u, t + 5, 1)
                            u = u + 2
                        out_p(t + 3)
                        if not last:
                            out_v(u)
                            u = u + 4
                        out_o(u, b)
                        if not last:
                            exps(t + 4, 0)

                    with act.Fori(0, B - 1) as b:
                        steps(b, False)
                    steps(B - 1, True)

                @block.gpsimd
                def _(pool):
                    for i in range(2):
                        for k in (k_hi[i], k_lo[i]):
                            pool.memset(k[SD:P, :, 0, :].bitcast(F32), 0.0)
                            m = pool.memset(k[0:SD, :, 1, :].bitcast(F32), 0.0)
                    m.then_inc(zeroed, 1)
                    pool.wait_ge(const_loaded, 48)

                    def turn_at(b, g):
                        par = g % 2
                        pool.wait_ge(swapped[par], 128 * b + 64 * (g // 2) + 64)
                        pool.tensor_tensor(qks[par][:], qks[par][:], cos[:].unsqueeze(1).to_broadcast((P, 4, T)), ALU.mult)
                        pool.tensor_tensor(qk[par][:], qk[par][:], ssin[:].unsqueeze(1).to_broadcast((P, 4, T)), ALU.mult).then_inc(turned, 1)

                    def steps(b, last):
                        turn_at(b, 2)
                        turn_at(b, 3)
                        if not last:
                            turn_at(b + 1, 0)
                            turn_at(b + 1, 1)
                        pool.wait_ge(xres_loaded, 16 * b + 16)
                        pool.tensor_tensor(xres[:], xres[:], obias[:].unsqueeze(1).to_broadcast((HT, 2, D)), ALU.add).then_inc(xres_ready, 1)

                    turn_at(0, 0)
                    turn_at(0, 1)
                    with pool.Fori(0, B - 1) as b:
                        steps(b, False)
                    steps(B - 1, True)

                @block.vector
                def _(dve):
                    dve.wait_ge(const_loaded, 48)

                    def norm(b):
                        dve.wait_ge(x_loaded, 16 * b + 16)
                        layer_norm_steps(dve, gate, ln, LN_STEPS * b, stats, mv, lnw, [xt[:, 0, :], xt[:, 1, :]],
                                         [xt[:, 0, :], xt[:, 1, :]])

                    def split_x(u):
                        dve.wait_ge(pj_free, u + 2)
                        dve.tensor_copy(xT_hi[:], xraw[:]).then_inc(mxd, 1)

                    def split_x2(m):
                        dve.wait_ge(mxd, m)
                        dve.tensor_tensor(xT_lo[:], xraw[:], xT_hi[:].bitcast(F32), ALU.subtract).then_inc(xT_ready, 1)

                    def rotate(t, g):
                        par = g % 2
                        dve.wait_ge(turned, t + 1)
                        if not (isinstance(t, int) and t < 2):
                            dve.wait_ge(s_full, 4 * t - 4)
                        dve.tensor_tensor(qk[par][:], qk[par][:], qks[par][:], ALU.add).then_inc(rope, 1)
                        dve.wait_ge(rope, 3 * t + 1)
                        q, k = qk[par][:, 0:2, :], qk[par][:, 2:4, :]
                        dve.tensor_copy(q_hi[par][:], q)
                        dve.tensor_copy(k_hi[par][0:SD, :, 0, :], k[0:SD])
                        dve.tensor_copy(k_hi[par][SD:P, :, 1, :], k[SD:P]).then_inc(rope, 1)
                        dve.wait_ge(rope, 3 * t + 2)
                        dve.tensor_tensor(q_lo[par][:], q, q_hi[par][:].bitcast(F32), ALU.subtract)
                        dve.tensor_tensor(k_lo[par][0:SD, :, 0, :], k[0:SD], k_hi[par][0:SD, :, 0, :].bitcast(F32), ALU.subtract)
                        dve.tensor_tensor(k_lo[par][SD:P, :, 1, :], k[SD:P], k_hi[par][SD:P, :, 1, :].bitcast(F32), ALU.subtract).then_inc(rope, 1)
                        dve.wait_ge(rope, 3 * t + 3)
                        dve.nop().then_inc(qk_ready, 1)

                    def mask_max(t, j):
                        n = 4 * t + j
                        dve.wait_ge(s_full, n + 1)
                        if not (isinstance(t, int) and t == 0):
                            dve.wait_ge(p_ready, n - 3)
                        dve.sem_inc(gate, 1)
                        for h in range(2):
                            w = HT * (h + 1)
                            m = dve.tensor_tensor_reduce(sm[:, j, h * HT:h * HT + w], psS[j % 2][0:HT, h * T:h * T + w], mask[:, h, 0:w],
                                                         1.0, NEG, ALU.add, ALU.max, mx[:, j, h:h + 1])
                        m.then_inc(mxd, 1)

                    def negate(t, j, m):
                        dve.wait_ge(mxd, m)
                        dve.tensor_scalar(nm[:, j, :], mx[:, j, :], -SD ** -0.5, None, ALU.mult).then_inc(sm_ready, 1)

                    def normalise(t, j):
                        n = 4 * t + j
                        dve.wait_ge(p_ready, n + 1)
                        dve.reciprocal(rs[:, j, :], sums[:, j, :]).then_inc(recip, 1)
                        dve.wait_ge(recip, n + 1)
                        dve.tensor_scalar(pr[:, j, 0:HT], pr[:, j, 0:HT], rs[:, j, 0:1], None, ALU.mult)
                        dve.tensor_scalar(pr[:, j, HT:3 * HT], pr[:, j, HT:3 * HT], rs[:, j, 1:2], None, ALU.mult).then_inc(pn_ready, 1)

                    def soft(t, m):
                        for j in range(4):
                            mask_max(t, j)
                            negate(t, j, m + j + 1)
                            if j >= 2:
                                normalise(t, j - 2)
                        normalise(t, 2)
                        normalise(t, 3)

                    def out_y(t, g):
                        dve.wait_ge(y_full, t + 1)
                        dve.tensor_copy(yT[:, 2 * g:2 * g + 2, :], psY[g % 2][:, 0:2 * T].rearrange("p (i t) -> p i t", i=2)).then_inc(y_ready, 1)

                    def residual(u, b):
                        dve.wait_ge(pj_free, u + 2)
                        dve.wait_ge(xres_ready, b + 1)
                        dve.tensor_tensor(osb[:], osb[:], xres[:], ALU.add).then_inc(o_ready, 1)

                    norm(0)
                    split_x(0)
                    split_x2(1)
                    rotate(0, 0)
                    rotate(1, 1)
                    norm(1)
                    soft(0, 1)

                    MX = 17

                    def steps(b, last, ahead):
                        t, u, m = 4 * b, PRE + PER * b, 5 + MX * b
                        soft(t + 1, m)
                        out_y(t, 0)
                        rotate(t + 2, 2)
                        soft(t + 2, m + 4)
                        out_y(t + 1, 1)
                        u = u + 4
                        if not last:
                            split_x(u)
                            split_x2(m + 9)
                            u = u + 2
                        rotate(t + 3, 3)
                        out_y(t + 2, 2)
                        if not last:
                            u = u + 2
                            soft(t + 3, m + 9)
                            rotate(t + 4, 0)
                            u = u + 6
                        else:
                            soft(t + 3, m + 8)
                        out_y(t + 3, 3)
                        if not last:
                            rotate(t + 5, 1)
                        if ahead:
                            norm(b + 2)
                        residual(u, b)
                        if not last:
                            soft(t + 4, m + 13)

                    with dve.Fori(0, B - 2) as b:
                        steps(b, False, True)
                    steps(B - 2, False, False)
                    steps(B - 1, True, False)


def constants():
    c = np.zeros((P, 1024), np.float32)
    c[:, 0:P] = np.eye(P)
    f = np.float32
    p = np.arange(32, dtype=f) / f(31)
    pos = np.arange(T, dtype=f)[None, :] / (f(10000.0) ** p)[:, None].astype(f)
    s, co = np.sin(pos).astype(f), np.cos(pos).astype(f)
    c[:, 128:352] = np.concatenate([s, -s, s, -s])
    c[:, 352:576] = np.concatenate([co] * 4)
    q = np.arange(HT)[:, None]
    k = np.arange(T)[None, :]
    c[0:HT, 576:800] = np.where(k <= q, 0, NEG)
    c[0:HT, 800:1024] = np.where(k <= q + HT, 0, NEG)
    return c


S2, C = 750, 384
KB = 6
KR = S2 // KB
CD = C // P
XH, XD = 16, 32
HALF = S2 // 2
KHALF = (slice(0, 376), slice(376, 750))
SHALF = (slice(0, 376), slice(374, 750))
BIG = float(2.0 ** 100)
ONE_ROW = 3 * XD


def cross_attention(nc, x1, ctx, cmask, w_q, w_k, w_v, w_o, cst, x2):
    with ExitStack() as outer:
        def sb(stack, name, shape, dt=F32):
            return stack.enter_context(nc.sbuf_tensor(name, shape, dt))

        def sem(name):
            return outer.enter_context(nc.semaphore(name))

        wq = [sb(outer, f"wq{i}", [P, KD, D], F32R) for i in range(2)]
        wk = [sb(outer, f"wk{i}", [P, CD, D], F32R) for i in range(2)]
        wv = [sb(outer, f"wv{i}", [P, CD, D], F32R) for i in range(2)]
        wo = sb(outer, "wo", [P, KD, D])
        ident = sb(outer, "x_ident", [P, P])

        with ExitStack() as c:
            raws = [sb(c, f"x_raw{i}", [P, n, D]) for i, n in enumerate((KD, CD, CD))]
            w_loaded = [sem(f"xw_loaded{i}") for i in range(4)]
            w_hi, w_lo = sem("xw_high"), sem("xw_low")
            with nc.Block() as block:
                @block.sync
                def _(sp):
                    for i, w in enumerate((w_q, w_k, w_v)):
                        sp.dma_start(raws[i][:], w.rearrange("(k p) n -> p k n", p=P)).then_inc(w_loaded[i], 16)
                    sp.dma_start(wo[:], w_o.rearrange("(k p) n -> p k n", p=P)).then_inc(w_loaded[3], 16)
                    sp.dma_start(ident[:], cst[:, 0:P]).then_inc(w_loaded[3], 16)
                    sp.wait_ge(w_loaded[3], 32)

                @block.scalar
                def _(act):
                    for i, w in enumerate((wq, wk, wv)):
                        act.wait_ge(w_loaded[i], 16)
                        act.activation(w[0][:], raws[i][:], ACT.Copy).then_inc(w_hi, 1)

                @block.vector
                def _(dve):
                    for i, w in enumerate((wq, wk, wv)):
                        dve.wait_ge(w_hi, i + 1)
                        dve.tensor_tensor(w[1][:], raws[i][:], w[0][:].bitcast(F32), ALU.subtract).then_inc(w_lo, 1)

        with ExitStack() as c:
            xt, xres, osb = (sb(c, n, [HT, 2, D]) for n in ("x_xt", "x_xres", "x_osb"))
            stats, mv, lnw = sb(c, "x_stats", [HT, 2, 6]), sb(c, "x_mv", [HT, 2, 2]), sb(c, "x_lnw", [HT, 8])
            ctxt = sb(c, "ctxt", [KR, KB, C])
            raw = [sb(c, f"raw{i}", [P, 512]) for i in range(4)]
            xT = [sb(c, f"x_xT{i}", [P, KD, T], F32R) for i in range(2)]
            cT = [sb(c, f"cT{i}", [P, CD, S2], F32R) for i in range(2)]
            qT = [sb(c, f"qT{i}", [P, KD, T], F32R) for i in range(2)]
            kT = [sb(c, f"kT{i}", [P, S2], F32R) for i in range(2)]
            q_st = sb(c, "q_st", [P, XH, T], F32R)
            k_st = [sb(c, f"k_st{i}", [P, S2], F32R) for i in range(8)]
            v = sb(c, "x_v", [KR, KB, D])
            ones = sb(c, "x_ones", [KR, XD])
            mk8 = sb(c, "mk8", [P, S2], mybir.dt.uint8)
            valid = sb(c, "valid", [P, 1])
            mk = sb(c, "mk", [P, S2])
            mrow = sb(c, "mrow", [P, S2], F32R)
            mx2 = sb(c, "x_mx2", [HT, 4, 2, 2])
            mx, m3 = sb(c, "x_mx", [HT, 4, 2]), sb(c, "m3", [HT, 4, 2, 3], F32R)
            pt = [sb(c, f"x_pt{i}", [KR, 3, 2 * T]) for i in range(4)]
            part = sb(c, "part", [KR, 2 * T])
            ptsum = [sb(c, f"ptsum{i}", [KR, T]) for i in range(4)]
            yT, sT = sb(c, "x_yT", [P, KD, T]), sb(c, "x_sT", [P, KD, T])
            pj = [c.enter_context(nc.psum_tensor(f"x_pj{i}", [P, 512], F32)) for i in range(2)]
            psS = c.enter_context(nc.psum_tensor("x_psS", [P, 2, 512], F32))
            psE = [c.enter_context(nc.psum_tensor(f"x_psE{i}", [P, 512], F32)) for i in range(3)]
            psYZ = c.enter_context(nc.psum_tensor("x_psYZ", [P, 512], F32))
            psY, psZ = psYZ[:, 0:T], psYZ[:, T:2 * T]

            names = ("gate", "filled", "zeroed", "x_loaded", "c_loaded", "m_loaded", "m_valid", "xres_loaded", "stored", "ln",
                     "pj_full", "pj_free", "raw_used",
                     "s_full", "s_taken", "m_parts", "m_ready", "st_full", "exp_done", "pv_done",
                     "y_out", "y_norm", "mstep", "part", "pt_summed", "m_joined")
            S = {n: sem("x_" + n) for n in names}
            k_placed = [sem(f"k_placed{j}") for j in range(4)]
            q_placed = [sem(f"q_placed{j}") for j in range(2)]

            xv = x1.rearrange("(b h p) d -> b p h d", p=HT, h=2)
            ov = x2.rearrange("(b h p) d -> b p h d", p=HT, h=2)
            cv = ctx.rearrange("b (k p) d -> b p k d", p=KR)

            def at(view, b, pat):
                return view[b] if isinstance(b, int) else view[bass.ds(b, 1)].rearrange(pat)

            def is_below(n, k):
                return isinstance(n, int) and n < k

            class Count:
                def __init__(self, base, offset):
                    self.base, self.k, self.offset = base, 0, offset

                def next(self):
                    self.k += 1
                    return self.base + (self.k - 1), self.offset + self.k - 1

                def skip(self, n):
                    self.k += n

            def used(kind, b, g=0, last=False):
                if is_below(b, 1) and (kind in ("x", "ctx", "q") or kind == "k" and g < 2):
                    return {"x": 2, "ctx": 8, "q": 10, "k": 12 + 2 * g}[kind]
                if kind == "out":
                    return RPRE + RPER * b + (6 if last else RPER)
                return RPER * b + {"x": -2, "ctx": 6, "q": 8, "k": (10, 12, 16, 18 if last else 20)[g]}[kind]

            PRE, PER = 20, 34
            RPRE, RPER = 14, 20
            SPRE, SPER = 14, 18

            with nc.Block() as block:
                @block.sync
                def _(sp):
                    def load(b):
                        sp.dma_start(xt[:], at(xv, b, "o p h d -> (o p) h d")).then_inc(S["x_loaded"], 16)

                    def load_ctx(b):
                        if not is_below(b, 1):
                            hold(sp, S["gate"], S["m_valid"], 2 * b)
                        sp.dma_start(ctxt[:], at(cv, b, "o p k d -> (o p) k d")).then_inc(S["c_loaded"], 16)
                        sp.dma_start(mk8[:], cmask[b:b + 1, :].to_broadcast((P, S2)) if isinstance(b, int)
                                     else cmask[bass.ds(b, 1), :].to_broadcast((P, S2))).then_inc(S["m_loaded"], 16)

                    def place_k(t, b, g, last=False):
                        hold(sp, S["gate"], S["raw_used"], used("k", b, g, last))
                        hold(sp, S["gate"], S["m_valid"], 2 * b + 2)
                        for j in range(4):
                            if not is_below(t, 2):
                                hold(sp, S["gate"], S["st_full"], 12 * t - 21 + 3 * j)
                            slot = k_st[4 * (g % 2) + j]
                            rows = slice(32 * j, 32 * j + 32)
                            sp.dma_start(slot[0:32, :].bitcast(F32), kT[0][rows, :].bitcast(F32)).then_inc(k_placed[j], 16)
                            sp.dma_start(slot[32:64, :].bitcast(F32), kT[1][rows, :].bitcast(F32)).then_inc(k_placed[j], 16)
                            sp.dma_start(slot[64:96, :].bitcast(F32), kT[0][rows, :].bitcast(F32)).then_inc(k_placed[j], 16)
                            sp.dma_start(slot[96:97, :].bitcast(F32), mrow[96:97, :].bitcast(F32)).then_inc(k_placed[j], 16)

                    def place_q(b, half):
                        hold(sp, S["gate"], S["raw_used"], used("q", b))
                        if not is_below(b, 1):
                            hold(sp, S["gate"], S["st_full"], 48 * b - 24 + 24 * half)
                        for j in range(4):
                            rows = slice(32 * j, 32 * j + 32)
                            for s, part in enumerate((0, 0, 1)):
                                sp.dma_start(q_st[32 * s:32 * s + 32, 8 * half + j:8 * half + 8:4, :].bitcast(F32),
                                             qT[part][rows, 2 * half:2 * half + 2, :].bitcast(F32)).then_inc(q_placed[half], 16)

                    def steps(b, last, ahead):
                        t = 4 * b
                        if not last:
                            load_ctx(b + 1)
                        place_k(t + 2, b, 2)
                        place_k(t + 3, b, 3, last)
                        if ahead:
                            load(b + 2)
                        if not last:
                            place_q(b + 1, 0)
                            place_k(t + 4, b + 1, 0)
                            place_k(t + 5, b + 1, 1)
                            place_q(b + 1, 1)
                        hold(sp, S["gate"], S["raw_used"], used("out", b, last=last))
                        sp.dma_start(at(ov, b, "o p h d -> (o p) h d"), osb[:]).then_inc(S["stored"], 16)
                        hold(sp, S["gate"], S["stored"], 16 * b + 16)
                        if not last:
                            load_res(b + 1)

                    def load_res(b):
                        sp.dma_start(xres[:], at(xv, b, "o p h d -> (o p) h d")).then_inc(S["xres_loaded"], 16)

                    load(0)
                    load_ctx(0)
                    load_res(0)
                    hold(sp, S["gate"], S["zeroed"], 1)
                    place_q(0, 0)
                    load(1)
                    place_q(0, 1)
                    place_k(0, 0, 0)
                    place_k(1, 0, 1)
                    with sp.Fori(0, B - 2) as b:
                        steps(b, False, True)
                    steps(B - 2, False, False)
                    steps(B - 1, True, False)

                @block.gpsimd
                def _(pool):
                    fills = [ones[:], m3[:].bitcast(F32), q_st[96:99, :, :].bitcast(F32)] + [k[96:99, :].bitcast(F32) for k in k_st]
                    for n, f in enumerate(fills):
                        pool.memset(f, 1.0).then_inc(S["filled"], 1)
                        pool.wait_ge(S["filled"], n + 1)
                    pool.nop().then_inc(S["zeroed"], 1)

                    def sum_blocks(t):
                        for j in range(4):
                            n = 4 * t + j
                            pool.wait_ge(S["exp_done"], 3 * n + 3)
                            pool.tensor_tensor(part[:], pt[j][:, 0, :], pt[j][:, 1, :], ALU.add).then_inc(S["part"], 1)
                            pool.wait_ge(S["part"], 2 * n + 1)
                            pool.tensor_tensor(part[:], part[:], pt[j][:, 2, :], ALU.add).then_inc(S["part"], 1)
                            pool.wait_ge(S["part"], 2 * n + 2)
                            pool.tensor_tensor(ptsum[j][:], part[:, 0:T], part[:, T:2 * T], ALU.add).then_inc(S["pt_summed"], 1)
                            pool.wait_ge(S["pt_summed"], n + 1)

                    with pool.Fori(0, 4 * B) as t:
                        sum_blocks(t)

                @block.tensor
                def _(pe):
                    def unit(u):
                        n, k = u.next()
                        if not is_below(n, 2):
                            pe.wait_ge(S["pj_free"], n - 1)
                        return pj[k % 2]

                    def turn_x(u, b):
                        pe.wait_ge(S["ln"], LN_STEPS * b + LN_STEPS)
                        for h in range(2):
                            o = unit(u)
                            for k in range(KD):
                                m = pe.transpose(o[:, k * HT:(k + 1) * HT], xt[:, h, k * P:(k + 1) * P], ident[0:HT, 0:HT])
                            m.then_inc(S["pj_full"], 1)

                    def turn_ctx(u, b):
                        pe.wait_ge(S["c_loaded"], 16 * b + 16)
                        for k in range(CD):
                            for s in range(2):
                                o = unit(u)
                                for i in range(3):
                                    m = pe.transpose(o[:, i * KR:(i + 1) * KR], ctxt[:, 3 * s + i, k * P:(k + 1) * P],
                                                     ident[0:KR, 0:KR])
                                m.then_inc(S["pj_full"], 1)

                    def project_q(u, b):
                        pe.wait_ge(S["raw_used"], used("x", b))
                        for s in range(2):
                            o = unit(u)
                            for i in range(2):
                                cols = slice((2 * s + i) * P, (2 * s + i + 1) * P)
                                for k in range(KD):
                                    m = mm3(pe, o[:, i * T:(i + 1) * T], (wq[0][:, k, cols], wq[1][:, k, cols]),
                                            (xT[0][:, k, :], xT[1][:, k, :]), k == 0, k == KD - 1)
                            m.then_inc(S["pj_full"], 1)

                    def project_k(u, g, s):
                        o = unit(u)
                        cols, rows = slice(g * P, (g + 1) * P), KHALF[s]
                        for k in range(CD):
                            m = mm3(pe, o[:, 0:rows.stop - rows.start], (wk[0][:, k, cols], wk[1][:, k, cols]),
                                    (cT[0][:, k, rows], cT[1][:, k, rows]), k == 0, k == CD - 1)
                        m.then_inc(S["pj_full"], 1)

                    def project_v(u, blocks=range(KB)):
                        for r in blocks:
                            o = unit(u)
                            for k in range(CD):
                                m = mm3(pe, o[0:KR, :], (cT[0][:, k, r * KR:(r + 1) * KR], cT[1][:, k, r * KR:(r + 1) * KR]),
                                        (wv[0][:, k, :], wv[1][:, k, :]), k == 0, k == CD - 1)
                            m.then_inc(S["pj_full"], 1)

                    def project_out(u, b):
                        pe.wait_ge(S["y_norm"], 4 * b + 4)
                        for h in range(2):
                            o = unit(u)
                            for k in range(KD):
                                m = pe.matmul(o[0:HT, :], yT[:, k, h * HT:(h + 1) * HT], wo[:, k, :],
                                              start=(k == 0), stop=(k == KD - 1))
                            m.then_inc(S["pj_full"], 1)

                    def turn_max(u, t, i):
                        o = unit(u)
                        pe.wait_ge(S["m_ready"], t + 1)
                        for j in range(2):
                            for h in range(2):
                                m = pe.matmul(o[96:99, j * T + h * HT:j * T + (h + 1) * HT], m3[:, 2 * i + j, h, :].bitcast(F32),
                                              ident[0:HT, 0:HT], start=True, stop=True)
                        m.then_inc(S["pj_full"], 1)
                        return u.base + u.k

                    def scores(t, g, j, h):
                        head = 4 * g + j
                        for s in range(2):
                            n = 16 * t + 4 * j + 2 * h + s
                            if not is_below(n, 2):
                                pe.wait_ge(S["s_taken"], n - 1)
                            pe.matmul(psS[0:HT, s, 0:376], q_st[0:97, head, h * HT:(h + 1) * HT],
                                      k_st[4 * (g % 2) + j][0:97, SHALF[s]], start=True, stop=True).then_inc(S["s_full"], 1)

                    def shifted(t, g, j):
                        n = 4 * t + j
                        for i in range(3):
                            if j:
                                pe.wait_ge(S["exp_done"], 3 * n + i - 2)
                            for s in range(2):
                                r = 2 * i + s
                                m = pe.matmul(psE[i][0:KR, s * T:(s + 1) * T], k_st[4 * (g % 2) + j][0:99, r * KR:(r + 1) * KR],
                                              q_st[0:99, 4 * g + j, :], start=True, stop=True)
                            m.then_inc(S["st_full"], 1)

                    def values(t, g, blocks):
                        if 0 in blocks:
                            pe.wait_ge(S["exp_done"], 12 * t + 12)
                            if g:
                                pe.wait_ge(S["y_out"], t)
                        for r in blocks:
                            for j in range(4):
                                head = 4 * g + j
                                pe.matmul(psY[32 * j:32 * j + 32, 0:T], v[:, r, head * XD:(head + 1) * XD],
                                          pt[j][:, r // 2, (r % 2) * T:(r % 2 + 1) * T],
                                          start=(r == 0), stop=(r == KB - 1))

                    def totals(t):
                        pe.wait_ge(S["pt_summed"], 4 * t + 4)
                        for j in range(4):
                            m = pe.matmul(psZ[32 * j:32 * j + 32, 0:T], ones[:], ptsum[j][:], start=True, stop=True)
                        m.then_inc(S["pv_done"], 1)

                    def step(u, t, g, prev, nxt, cur=True):
                        gp, gn = (g + 3) % 4, (g + 1) % 4

                        def unit_of_scores(n):
                            if cur:
                                if n % 2 == 0:
                                    pe.wait_ge(k_placed[n // 2], 64 * t + 64)
                                scores(t, g, n // 2, n % 2)

                        copied = []
                        for i in range(2):
                            unit_of_scores(i)
                            if nxt:
                                project_k(u, gn, i)
                            if prev and i == 1 and g != 1:
                                totals(t - 2)
                            if prev:
                                copied.append(turn_max(u, t - 1, i))
                        unit_of_scores(2)
                        if prev:
                            pe.wait_ge(S["pj_free"], copied[0])
                            shifted(t - 1, gp, 0)
                        unit_of_scores(3)
                        if prev:
                            shifted(t - 1, gp, 1)
                        unit_of_scores(4)
                        if prev:
                            pe.wait_ge(S["pj_free"], copied[1])
                            shifted(t - 1, gp, 2)
                        unit_of_scores(5)
                        if prev:
                            shifted(t - 1, gp, 3)
                        unit_of_scores(6)
                        if prev:
                            values(t - 1, gp, range(0, 3))
                        unit_of_scores(7)
                        if prev:
                            values(t - 1, gp, range(3, KB))

                    pe.wait_ge(S["zeroed"], 1)
                    u = Count(0, 0)
                    turn_x(u, 0)
                    turn_ctx(u, 0)
                    project_q(u, 0)
                    pe.wait_ge(S["raw_used"], used("ctx", 0))
                    project_k(u, 0, 0)
                    project_k(u, 0, 1)
                    pe.wait_ge(q_placed[0], 192)
                    step(u, 0, 0, False, True)
                    project_v(u)

                    def steps(b, last):
                        t, u = 4 * b, Count(PRE + PER * b, PRE)
                        pe.wait_ge(S["pj_free"], PRE + PER * b)
                        step(u, t + 1, 1, True, True)
                        if not last:
                            turn_x(u, b + 1)
                        pe.wait_ge(q_placed[1], 192 * b + 192)
                        step(u, t + 2, 2, True, True)
                        if not last:
                            turn_ctx(u, b + 1)
                            project_q(u, b + 1)
                            pe.wait_ge(S["raw_used"], used("ctx", b + 1))
                        step(u, t + 3, 3, True, not last)
                        if not last:
                            pe.wait_ge(q_placed[0], 192 * b + 384)
                            step(u, t + 4, 0, True, True)
                            project_v(u, range(0, 2))
                            totals(t + 3)
                            project_v(u, range(2, KB))
                        else:
                            step(u, t + 4, 0, True, False, False)
                            totals(t + 3)
                        project_out(u, b)

                    with pe.Fori(0, B - 1) as b:
                        steps(b, False)
                    steps(B - 1, True)

                @block.scalar
                def _(act):
                    def out_raw(u, r, rows, cols):
                        n, k = u.next()
                        rn, rk = r.next()
                        act.wait_ge(S["pj_full"], n + 1)
                        if not is_below(rn, 4):
                            act.wait_ge(S["raw_used"], rn - 3)
                        act.activation(raw[rk % 4][0:rows, 0:cols], pj[k % 2][0:rows, 0:cols], ACT.Copy).then_inc(S["pj_free"], 1)

                    def out_v(u, blocks=range(KB)):
                        for r in blocks:
                            n, k = u.next()
                            act.wait_ge(S["pj_full"], n + 1)
                            act.activation(v[:, r, :], pj[k % 2][0:KR, :], ACT.Copy).then_inc(S["pj_free"], 1)

                    def out_max(u, g, i):
                        n, k = u.next()
                        act.wait_ge(S["pj_full"], n + 1)
                        act.activation(q_st[96:99, 4 * g + 2 * i:4 * g + 2 * i + 2, :],
                                       pj[k % 2][96:99, 0:2 * T].rearrange("p (j t) -> p j t", j=2), ACT.Copy).then_inc(S["pj_free"], 1)

                    def exps(t, j):
                        n = 4 * t + j
                        for i in range(3):
                            act.wait_ge(S["st_full"], 3 * n + i + 1)
                            act.activation(pt[j][:, i, :], psE[i][0:KR, 0:2 * T], ACT.Exp, scale=XD ** -0.5).then_inc(S["exp_done"], 1)

                    def out_y(t, g):
                        act.wait_ge(S["pv_done"], t + 1)
                        act.activation(sT[:, g, :], psZ[:, 0:T], ACT.Copy)
                        act.activation(yT[:, g, :], psY[:, 0:T], ACT.Copy).then_inc(S["y_out"], 1)

                    def step(u, r, t, g, prev, nxt):
                        gp = (g + 3) % 4
                        if nxt:
                            out_raw(u, r, P, 376)
                        if prev:
                            out_max(u, gp, 0)
                        if nxt:
                            out_raw(u, r, P, 374)
                        if prev and g != 1:
                            out_y(t - 2, (g + 2) % 4)
                        if prev:
                            out_max(u, gp, 1)
                            for j in range(4):
                                exps(t - 1, j)

                    u, r = Count(0, 0), Count(0, 0)
                    for _i in range(2):
                        out_raw(u, r, P, 4 * HT)
                    for _i in range(6):
                        out_raw(u, r, P, HALF)
                    for _i in range(2):
                        out_raw(u, r, P, 2 * T)
                    out_raw(u, r, P, 376)
                    out_raw(u, r, P, 374)
                    step(u, r, 0, 0, False, True)
                    out_v(u)

                    def steps(b, last):
                        t, u, r = 4 * b, Count(PRE + PER * b, PRE), Count(RPRE + RPER * b, RPRE)
                        step(u, r, t + 1, 1, True, True)
                        if not last:
                            out_raw(u, r, P, 4 * HT)
                            out_raw(u, r, P, 4 * HT)
                        step(u, r, t + 2, 2, True, True)
                        if not last:
                            for _i in range(6):
                                out_raw(u, r, P, HALF)
                            out_raw(u, r, P, 2 * T)
                            out_raw(u, r, P, 2 * T)
                        step(u, r, t + 3, 3, True, not last)
                        step(u, r, t + 4, 0, True, not last)
                        if not last:
                            out_v(u, range(0, 2))
                        out_y(t + 3, 3)
                        if not last:
                            out_v(u, range(2, KB))
                        out_raw(u, r, HT, 512)
                        out_raw(u, r, HT, 512)

                    with act.Fori(0, B - 1) as b:
                        steps(b, False)
                    steps(B - 1, True)

                @block.vector
                def _(dve):
                    dve.wait_ge(S["zeroed"], 1)

                    def norm(b):
                        dve.wait_ge(S["x_loaded"], 16 * b + 16)
                        layer_norm_steps(dve, S["gate"], S["ln"], LN_STEPS * b, stats, mv, lnw, [xt[:, 0, :], xt[:, 1, :]],
                                         [xt[:, 0, :], xt[:, 1, :]])

                    def mask(b):
                        dve.wait_ge(S["m_loaded"], 16 * b + 16)
                        if not is_below(b, 1):
                            for j in range(4):
                                dve.wait_ge(k_placed[j], 256 * b)
                        dve.tensor_copy(mk[:], mk8[:]).then_inc(S["mstep"], 1)
                        dve.wait_ge(S["mstep"], 2 * b + 1)
                        dve.tensor_reduce(valid[:], mk[:], AX.X, ALU.max).then_inc(S["m_valid"], 1)
                        dve.wait_ge(S["m_valid"], 2 * b + 1)
                        dve.tensor_scalar(mk[96:97, :], mk[96:97, :], BIG, -BIG, ALU.mult, ALU.add).then_inc(S["mstep"], 1)
                        dve.wait_ge(S["mstep"], 2 * b + 2)
                        dve.tensor_scalar(mrow[96:97, :], mk[96:97, :], valid[96:97, :], None, ALU.mult).then_inc(S["m_valid"], 1)

                    def take(r):
                        (n, k), (un, _k) = r.next(), r.units.next()
                        dve.wait_ge(S["pj_free"], un + 1)
                        return n, raw[k % 4]

                    def split(r, hi, lo, shape, scaled=None):
                        n, src = take(r)
                        sn, _k = r.splits.next()
                        src = src[:, 0:shape[0] * shape[1]].rearrange("p (a c) -> p a c", a=shape[0])
                        if scaled is not None:
                            dve.tensor_scalar(src, src, valid[:, 0:1], None, ALU.mult).then_inc(q_scaled, 1)
                            dve.wait_ge(q_scaled, scaled)
                        dve.tensor_copy(hi, src).then_inc(split_done, 1)
                        dve.wait_ge(split_done, sn + 1)
                        dve.tensor_tensor(lo, src, hi.bitcast(F32), ALU.subtract).then_inc(S["raw_used"], 1)

                    def split_x(r):
                        for h in range(2):
                            cols = slice(h * HT, (h + 1) * HT)
                            split(r, xT[0][:, :, cols], xT[1][:, :, cols], (KD, HT))

                    def split_ctx(r):
                        for k in range(CD):
                            for s in range(2):
                                cols = slice(s * HALF, (s + 1) * HALF)
                                split(r, cT[0][:, k:k + 1, cols], cT[1][:, k:k + 1, cols], (1, HALF))

                    def split_q(r, b):
                        dve.wait_ge(S["m_valid"], 2 * b + 2)
                        if not is_below(b, 1):
                            dve.wait_ge(q_placed[1], 192 * b)
                        for s in range(2):
                            split(r, qT[0][:, 2 * s:2 * s + 2, :], qT[1][:, 2 * s:2 * s + 2, :], (2, T), 2 * b + s + 1)

                    def split_k(r, t, s):
                        if s == 0 and not is_below(t, 1):
                            for j in range(4):
                                dve.wait_ge(k_placed[j], 64 * t)
                        cols = KHALF[s]
                        split(r, kT[0][:, cols].unsqueeze(1), kT[1][:, cols].unsqueeze(1), (1, cols.stop - cols.start))

                    def maxima(t, lo, hi_):
                        if lo == 0 and not is_below(t, 1):
                            dve.wait_ge(S["m_ready"], t)
                        for n in range(lo, hi_):
                            j, h = divmod(n, 2)
                            for s in range(2):
                                dve.wait_ge(S["s_full"], 16 * t + 2 * n + s + 1)
                                dve.tensor_reduce(mx2[:, j, h, s:s + 1], psS[0:HT, s, 0:376], AX.X, ALU.max).then_inc(S["s_taken"], 1)
                        if hi_ == 8:
                            dve.wait_ge(S["s_taken"], 16 * t + 16)
                            dve.tensor_tensor(mx[:], mx2[:, :, :, 0], mx2[:, :, :, 1], ALU.max).then_inc(S["m_joined"], 1)
                            dve.wait_ge(S["m_joined"], t + 1)
                            dve.tensor_scalar(m3[:, :, :, 1], mx[:], -1.0, None, ALU.mult).then_inc(S["m_parts"], 1)
                            dve.wait_ge(S["m_parts"], t + 1)
                            dve.scalar_tensor_tensor(m3[:, :, :, 2], mx[:], -1.0, m3[:, :, :, 1].bitcast(F32), ALU.mult,
                                                     ALU.subtract).then_inc(S["m_ready"], 1)

                    def out_o(r, b):
                        dve.wait_ge(S["xres_loaded"], 16 * b + 16)
                        for h in range(2):
                            n, src = take(r)
                            dve.tensor_tensor(osb[:, h, :], src[0:HT, :], xres[:, h, :], ALU.add).then_inc(S["raw_used"], 1)

                    def norm_y(b):
                        for i, g in enumerate((slice(0, 3), slice(3, 4))):
                            dve.wait_ge(S["y_out"], 4 * b + 3 + i)
                            dve.reciprocal(sT[:, g, :], sT[:, g, :]).then_inc(S["y_norm"], 1)
                            dve.wait_ge(S["y_norm"], 4 * b + 2 * i + 1)
                            dve.tensor_tensor(yT[:, g, :], yT[:, g, :], sT[:, g, :], ALU.mult).then_inc(S["y_norm"], 1)

                    split_done = sem("split_done")
                    q_scaled = sem("q_scaled")

                    def rings(u, r, n):
                        c = Count(*r)
                        c.units, c.splits = Count(*u), Count(*n)
                        return c

                    def step(r, t, prev, nxt, cur=True):
                        for i in range(2):
                            if cur:
                                maxima(t, i, i + 1)
                            if nxt:
                                split_k(r, t + 1, i)
                            r.units.skip(int(prev))
                        if cur:
                            maxima(t, 2, 8)

                    r = rings((0, 0), (0, 0), (0, 0))
                    norm(0)
                    mask(0)
                    split_x(r)
                    split_ctx(r)
                    split_q(r, 0)
                    split_k(r, 0, 0)
                    split_k(r, 0, 1)
                    step(r, 0, False, True)
                    norm(1)

                    def steps(b, last, ahead):
                        t = 4 * b
                        r = rings((PRE + PER * b, PRE), (RPRE + RPER * b, RPRE), (SPRE + SPER * b, SPRE))
                        step(r, t + 1, True, True)
                        if not last:
                            split_x(r)
                        step(r, t + 2, True, True)
                        if not last:
                            mask(b + 1)
                            split_ctx(r)
                            split_q(r, b + 1)
                        step(r, t + 3, True, not last)
                        step(r, t + 4, True, not last, not last)
                        if not last:
                            r.units.skip(6)
                        norm_y(b)
                        if ahead:
                            norm(b + 2)
                        out_o(r, b)

                    with dve.Fori(0, B - 2) as b:
                        steps(b, False, True)
                    steps(B - 2, False, False)
                    steps(B - 1, True, False)


BF16 = mybir.dt.bfloat16
E = 8
F = 2048
CAP = int(1.25 * N / E)
SLOT_TILES = CAP // HT
NT = N // HT
XW = D + E
FT = F // P
CT = 8
CHUNKS = NT // CT
CHUNK_STEPS = 3 * CT + 19
RADIX_STEPS = 15

C_SAME, C_BEFORE, C_TRI, C_IOTA, C_HI, C_TOK, C_BITS = 1024, 1152, 1280, 1344, 1456, 1464, 1528
C_END = C_BITS + 3 * RADIX_STEPS


def routing_constants(c):
    e, b = np.arange(P) // B, np.arange(P) % B
    same = e[:, None] == e[None, :]
    c[:, C_SAME:C_SAME + P] = same
    c[:, C_BEFORE:C_BEFORE + P] = same & (b[:, None] < b[None, :])
    c[:, C_TRI:C_TRI + E * E] = (np.arange(E)[None, :] < np.arange(E)[:, None]).reshape(1, -1)
    c[:, C_IOTA:C_IOTA + HT] = np.arange(HT)
    c[:, C_HI:C_HI + SLOT_TILES] = np.arange(SLOT_TILES)
    h, t = np.arange(NT) // B, np.arange(NT) % B
    token = (T * t + HT * h)[None, :] + np.arange(P)[:, None] + 1
    c[:, C_TOK:C_TOK + NT] = token // 64 * 64
    c[:, C_TOK + NT:C_TOK + 2 * NT] = token % 64
    bits = np.array([k << (2 * s) for s in reversed(range(RADIX_STEPS)) for k in (1, 2, 3)], np.int32)
    c[:, C_BITS:C_END] = bits.view(np.float32)


def all_constants():
    c = np.zeros((P, C_END), np.float32)
    c[:, 0:1024] = constants()
    routing_constants(c)
    return c


def experts(nc, out, router_w, w_g, w_u, w_d, cst, rows_w):
    with ExitStack() as outer:
        def sb(stack, name, shape, dt=F32):
            return stack.enter_context(nc.sbuf_tensor(name, shape, dt))

        def sem(name):
            return outer.enter_context(nc.semaphore(name))

        def psum(stack, name):
            return stack.enter_context(nc.psum_tensor(name, [P, 512], F32))

        consts = sb(outer, "r_consts", [P, C_END - 1024])
        ident = sb(outer, "r_ident", [P, P])
        logits = sb(outer, "logits", [HT, NT, E])
        gather_rows = sb(outer, "gather_rows", [HT, E * SLOT_TILES], U32)
        scatter_rows = sb(outer, "scatter_rows", [HT, E * SLOT_TILES], U32)

        def const(start, n):
            return consts[:, start - 1024:start - 1024 + n]

        with ExitStack() as c:
            rw = sb(c, "rw", [E, D])
            rwT = sb(c, "rwT", [P, KD, E])
            xt = [sb(c, f"r_xt{i}", [HT, CT, D]) for i in range(2)]
            xnT = [sb(c, f"r_xnT{h}", [P, KD, HT]) for h in range(2)]
            stats, mv, lnw = sb(c, "r_stats", [HT, CT, 6]), sb(c, "r_mv", [HT, CT, 2]), sb(c, "r_lnw", [HT, 4 * CT])
            psX = [psum(c, f"r_psX{h}") for h in range(2)]
            psL = [psum(c, f"r_psL{i}") for i in range(2)]
            psR = psum(c, "r_psR")
            loaded = [sem(f"r_loaded{i}") for i in range(2)]
            stored = [sem(f"r_stored{i}") for i in range(2)]
            names = ("gate", "c_loaded", "ln", "rw_turned", "rw_out", "turned", "turn_out", "logits_done", "logits_out")
            gate, c_loaded, ln, rw_turned, rw_out, turned, turn_out, logits_done, logits_out = (sem("r_" + n) for n in names)
            xv = out.rearrange("(c t p) d -> c p t d", p=HT, t=CT)
            rv = rows_w.rearrange("(c t p) d -> c p t d", p=HT, t=CT)

            def at(view, b):
                return view[b] if isinstance(b, int) else view[bass.ds(b, 1)].rearrange("o p t d -> (o p) t d")

            with nc.Block() as block:
                @block.sync
                def _(sp):
                    sp.dma_start(consts[:], cst[:, 1024:C_END]).then_inc(c_loaded, 16)
                    sp.dma_start(ident[:], cst[:, 0:P]).then_inc(c_loaded, 16)
                    sp.dma_start(rw[:], router_w).then_inc(c_loaded, 16)
                    for b in range(2):
                        sp.dma_start(xt[b][:], at(xv, b)).then_inc(loaded[b], 16)

                    def store(q, i):
                        hold(sp, gate, ln, CHUNK_STEPS * (2 * q + i) + CHUNK_STEPS)
                        dst = rv[2 * q + i, :, :, 0:D] if isinstance(q, int) else \
                            rv[bass.ds(2 * q + i, 1), :, :, 0:D].rearrange("o p t d -> (o p) t d")
                        sp.dma_start(dst, xt[i][:]).then_inc(stored[i], 16)

                    with sp.Fori(0, CHUNKS // 2 - 1) as q:
                        for i in range(2):
                            store(q, i)
                            hold(sp, gate, stored[i], 16 * q + 16)
                            hold(sp, gate, turned, 2 * CT * q + CT * i + CT)
                            sp.dma_start(xt[i][:], at(xv, 2 * q + 2 + i)).then_inc(loaded[i], 16)
                    for i in range(2):
                        store(CHUNKS // 2 - 1, i)
                    for i in range(2):
                        sp.wait_ge(stored[i], 16 * (CHUNKS // 2))

                @block.vector
                def _(dve):
                    with dve.Fori(0, CHUNKS // 2) as q:
                        for i in range(2):
                            dve.wait_ge(loaded[i], 16 * q + 16)
                            tiles = [xt[i][:, t, :] for t in range(CT)]
                            layer_norm_steps(dve, gate, ln, CHUNK_STEPS * (2 * q + i), stats, mv, lnw, tiles, tiles)

                @block.tensor
                def _(pe):
                    pe.wait_ge(c_loaded, 48)
                    for k in range(KD):
                        m = pe.transpose(psR[:, k * E:(k + 1) * E], rw[:, k * P:(k + 1) * P], ident[0:E, 0:E])
                    m.then_inc(rw_turned, 1)

                    def turn(n, c, t, i, first):
                        pe.wait_ge(ln, CHUNK_STEPS * c + CHUNK_STEPS - CT + t + 1)
                        if not first:
                            pe.wait_ge(turn_out, n - 1)
                        for k in range(KD):
                            m = pe.transpose(psX[t % 2][:, k * HT:(k + 1) * HT], xt[i][:, t, k * P:(k + 1) * P], ident[0:HT, 0:HT])
                        m.then_inc(turned, 1)

                    def route(n, c, t, i, first):
                        pe.wait_ge(turn_out, n + 1)
                        if not first:
                            pe.wait_ge(logits_out, c)
                        for k in range(KD):
                            m = pe.matmul(psL[i][0:HT, t * E:(t + 1) * E], xnT[t % 2][:, k, :], rwT[:, k, :],
                                          start=(k == 0), stop=(k == KD - 1))
                        if t == CT - 1:
                            m.then_inc(logits_done, 1)

                    def chunk(c, i, first):
                        n = CT * c
                        for t in range(CT):
                            turn(n + t, c, t, i, first and t < 2)
                            if t:
                                route(n + t - 1, c, t - 1, i, first)
                        route(n + CT - 1, c, CT - 1, i, first)

                    pe.wait_ge(rw_out, 1)
                    chunk(0, 0, True)
                    chunk(1, 1, False)
                    with pe.Fori(1, CHUNKS // 2) as q:
                        for i in range(2):
                            chunk(2 * q + i, i, False)

                @block.scalar
                def _(act):
                    act.wait_ge(rw_turned, 1)
                    act.activation(rwT[:], psR[:, 0:KD * E].rearrange("p (k e) -> p k e", k=KD), ACT.Copy).then_inc(rw_out, 1)

                    with act.Fori(0, CHUNKS // 2) as q:
                        for i in range(2):
                            c = 2 * q + i
                            for t in range(CT):
                                act.wait_ge(turned, CT * c + t + 1)
                                act.activation(xnT[t % 2][:], psX[t % 2][:, 0:KD * HT].rearrange("p (k t) -> p k t", k=KD),
                                               ACT.Copy).then_inc(turn_out, 1)
                            act.wait_ge(logits_done, c + 1)
                            act.activation(logits[:, bass.ds(CT * c, CT), :], psL[i][0:HT, 0:CT * E].rearrange("p (t e) -> p t e", t=CT),
                                           ACT.Copy).then_inc(logits_out, 1)

        with ExitStack() as c:
            small, total, recip = (sb(c, "g_" + n, [HT, NT]) for n in ("small", "total", "recip"))
            prob, rank, weight = (sb(c, "g_" + n, [HT, NT, E]) for n in ("prob", "rank", "weight"))
            above, tied = (sb(c, "g_" + n, [HT, NT, E, E]) for n in ("above", "tied"))
            wsort = sb(c, "wsort", [HT, 2, E, B])
            w = sb(c, "g_w", [P, T])
            cand, chosen, count = sb(c, "cand", [P, 3]), sb(c, "chosen", [P, 4]), sb(c, "count", [P, 3])
            thr, more = sb(c, "thr", [P, 1]), sb(c, "more", [P, 1])
            hits = sb(c, "hits", [P, 3, T])
            gt, eq, keep, run, one, pos = (sb(c, "g_" + n, [P, T]) for n in ("gt", "eq", "keep", "run", "one", "pos"))
            sums = sb(c, "g_sums", [P, 3])
            base = sb(c, "g_base", [P, 3])
            posT, hi, lo = (sb(c, "g_" + n, [HT, 2 * P]) for n in ("posT", "hi", "lo"))
            onehi = sb(c, "onehi", [HT, 2 * P, SLOT_TILES])
            value = sb(c, "value", [HT, 2 * P, 2, SLOT_TILES], BF16)
            onelo = [sb(c, f"onelo{i}", [HT, B, HT], BF16) for i in range(2)]
            tab = sb(c, "tab", [HT, E, 2, SLOT_TILES])
            tok, row, skip = (sb(c, "g_" + n, [HT, E, SLOT_TILES]) for n in ("tok", "row", "skip"))
            psW, psC, psP, psQ, psB = (psum(c, "g_" + n) for n in ("psW", "psC", "psP", "psQ", "psB"))
            names = ("step", "shifted", "exped", "w_ready", "w_stored", "w_turned", "counted", "summed", "totals", "carried",
                     "placed", "pos_turned", "one_ready", "one_used", "tabled")
            step, shifted, exped, w_ready, w_stored, w_turned, counted, summed, totals, carried, placed, pos_turned, \
                one_ready, one_used, tabled = (sem("g_" + n) for n in names)

            with nc.Block() as block:
                @block.sync
                def _(sp):
                    sp.wait_ge(w_ready, 1)
                    sp.dma_start(rows_w.rearrange("(i p) d -> p i d", p=HT)[:, :, D:XW], weight[:]).then_inc(w_stored, 16)
                    sp.wait_ge(w_stored, 16)

                @block.scalar
                def _(act):
                    act.wait_ge(shifted, 1)
                    act.activation(prob[:], logits[:], ACT.Exp).then_inc(exped, 1)

                @block.tensor
                def _(pe):
                    pe.wait_ge(w_ready, 2)
                    for h in range(2):
                        m = pe.transpose(psW[:, h * HT:(h + 1) * HT], wsort[:, h, :, :].rearrange("p e b -> p (e b)"),
                                         ident[0:HT, 0:HT])
                    m.then_inc(w_turned, 1)
                    for s in range(RADIX_STEPS):
                        pe.wait_ge(counted, s + 1)
                        pe.matmul(psC[:, 0:3], const(C_SAME, P), count[:], start=True, stop=True).then_inc(summed, 1)
                    pe.wait_ge(totals, 1)
                    pe.matmul(psC[:, 4:5], const(C_SAME, P), sums[:, 0:1], start=True, stop=True)
                    pe.matmul(psC[:, 6:7], const(C_BEFORE, P), sums[:, 1:2], start=True, stop=True).then_inc(carried, 1)
                    pe.wait_ge(totals, 2)
                    pe.matmul(psC[:, 8:9], const(C_BEFORE, P), sums[:, 2:3], start=True, stop=True).then_inc(carried, 1)
                    pe.wait_ge(placed, 1)
                    for h in range(2):
                        m = pe.transpose(psP[0:HT, h * P:(h + 1) * P], pos[:, h * HT:(h + 1) * HT], ident[:])
                    m.then_inc(pos_turned, 1)
                    for e in range(E):
                        for h in range(2):
                            n = 2 * e + h
                            pe.wait_ge(one_ready, n + 1)
                            for b in range(B):
                                col = h * P + e * B + b
                                m = pe.matmul(psQ[0:HT, e * 10:(e + 1) * 10], onelo[h][:, b, :],
                                              value[:, col, :, :].rearrange("p v t -> p (v t)"),
                                              start=(h == 0 and b == 0), stop=(h == 1 and b == B - 1))
                            m.then_inc(one_used, 1)

                @block.vector
                def _(dve):
                    k = 0

                    def done(ins):
                        nonlocal k
                        k += 1
                        ins.then_inc(step, 1)
                        dve.wait_ge(step, k)

                    def over(t):
                        return t[:].unsqueeze(2).to_broadcast((HT, NT, E))

                    done(dve.tensor_reduce(small[:], logits[:], AX.X, ALU.max))
                    dve.tensor_tensor(logits[:], logits[:], over(small), ALU.subtract).then_inc(shifted, 1)
                    dve.wait_ge(exped, 1)
                    done(dve.tensor_reduce(total[:], prob[:], AX.X, ALU.add))
                    done(dve.reciprocal(recip[:], total[:]))
                    done(dve.tensor_tensor(prob[:], prob[:], over(recip), ALU.mult))
                    full = (HT, NT, E, E)
                    mine, other = prob[:].unsqueeze(3).to_broadcast(full), prob[:].unsqueeze(2).to_broadcast(full)
                    dve.tensor_tensor(above[:], other, mine, ALU.is_gt)
                    done(dve.tensor_tensor(tied[:], other, mine, ALU.is_equal))
                    tri = const(C_TRI, E * E)[0:HT].rearrange("p (e f) -> p e f", e=E).unsqueeze(1).to_broadcast(full)
                    done(dve.tensor_tensor(tied[:], tied[:], tri, ALU.mult))
                    done(dve.tensor_tensor(above[:], above[:], tied[:], ALU.add))
                    done(dve.tensor_reduce(rank[:], above[:], AX.X, ALU.add))
                    done(dve.scalar_tensor_tensor(weight[:], rank[:], 1.5, prob[:], ALU.is_lt, ALU.mult))
                    done(dve.tensor_reduce(total[:], weight[:], AX.X, ALU.add))
                    done(dve.tensor_scalar(total[:], total[:], 1e-6, None, ALU.add))
                    done(dve.reciprocal(recip[:], total[:]))
                    dve.tensor_tensor(weight[:], weight[:], over(recip), ALU.mult).then_inc(w_ready, 1)
                    dve.wait_ge(w_ready, 1)
                    wv = weight[:].rearrange("p (b h) e -> p h e b", h=2)
                    for h in range(2):
                        m = dve.tensor_copy(wsort[:, h, :, :], wv[:, h, :, :])
                    m.then_inc(w_ready, 1)

                    dve.memset(one[:], 1.0)
                    dve.memset(chosen[:], 0.0)
                    done(dve.memset(thr[:], 0.0))
                    dve.wait_ge(w_turned, 1)
                    done(dve.tensor_copy(w[:], psW[:, 0:T]))
                    for s in range(RADIX_STEPS):
                        bits = const(C_BITS + 3 * s, 3).bitcast(I32)
                        done(dve.tensor_tensor(cand[:].bitcast(I32), thr[:].bitcast(I32).to_broadcast((P, 3)), bits, ALU.bitwise_or))
                        for i in range(3):
                            m = dve.tensor_scalar(hits[:, i, :], w[:], cand[:, i:i + 1], 0.0, ALU.is_ge, ALU.add,
                                                  accum_out=count[:, i:i + 1])
                        m.then_inc(counted, 1)
                        dve.wait_ge(summed, s + 1)
                        done(dve.scalar_tensor_tensor(chosen[:, 1:4], psC[:, 0:3], CAP - 0.5, cand[:], ALU.is_ge, ALU.mult))
                        done(dve.tensor_reduce(thr[:], chosen[:], AX.X, ALU.max))
                        done(dve.tensor_copy(chosen[:, 0:1], thr[:]))

                    dve.tensor_scalar(gt[:], w[:], thr[:, 0:1], 0.0, ALU.is_gt, ALU.add, accum_out=sums[:, 0:1])
                    done(dve.tensor_scalar(eq[:], w[:], thr[:, 0:1], None, ALU.is_equal))
                    done(dve.scalar_tensor_tensor(eq[:], w[:], 0.0, eq[:], ALU.is_gt, ALU.mult))
                    done(dve.tensor_tensor_scan(run[:], one[:], eq[:], 0.0, ALU.mult, ALU.add))
                    dve.tensor_copy(sums[:, 1:2], run[:, T - 1:T]).then_inc(totals, 1)
                    dve.wait_ge(carried, 1)
                    done(dve.tensor_copy(base[:, 0:2], psC[:, 4:8:2]))
                    done(dve.tensor_tensor(more[:], base[:, 0:1], base[:, 1:2], ALU.add))
                    done(dve.tensor_scalar(run[:], run[:], more[:, 0:1], CAP + 0.5, ALU.add, ALU.is_lt))
                    done(dve.tensor_tensor(eq[:], eq[:], run[:], ALU.mult))
                    done(dve.tensor_tensor(keep[:], gt[:], eq[:], ALU.add))
                    done(dve.tensor_tensor_scan(run[:], one[:], keep[:], 0.0, ALU.mult, ALU.add))
                    dve.tensor_copy(sums[:, 2:3], run[:, T - 1:T]).then_inc(totals, 1)
                    dve.wait_ge(carried, 2)
                    done(dve.tensor_copy(base[:, 2:3], psC[:, 8:9]))
                    done(dve.scalar_tensor_tensor(pos[:], run[:], base[:, 2:3], keep[:], ALU.add, ALU.mult))
                    dve.tensor_scalar(pos[:], pos[:], -1.0, None, ALU.add).then_inc(placed, 1)
                    dve.wait_ge(pos_turned, 1)
                    done(dve.tensor_copy(posT[:], psP[0:HT, 0:2 * P]))
                    done(dve.tensor_scalar(hi[:], posT[:], float(HT), None, ALU.is_ge))
                    for t in range(2, SLOT_TILES):
                        done(dve.scalar_tensor_tensor(hi[:], posT[:], float(HT * t), hi[:], ALU.is_ge, ALU.add))
                    dve.scalar_tensor_tensor(lo[:], hi[:], -float(HT), posT[:], ALU.mult, ALU.add)
                    shape = (HT, 2 * P, SLOT_TILES)
                    done(dve.tensor_tensor(onehi[:], hi[:].unsqueeze(2).to_broadcast(shape),
                                           const(C_HI, SLOT_TILES)[0:HT].unsqueeze(1).to_broadcast(shape), ALU.is_equal))
                    for h in range(2):
                        for v in range(2):
                            token = const(C_TOK + v * NT + h * B, B)[0:HT].unsqueeze(1).unsqueeze(3)
                            shape = (HT, E, B, SLOT_TILES)
                            cols = slice(h * P, (h + 1) * P)
                            m = dve.tensor_tensor(value[:, cols, v, :].rearrange("p (e b) t -> p e b t", e=E),
                                                  onehi[:, cols, :].rearrange("p (e b) t -> p e b t", e=E),
                                                  token.to_broadcast(shape), ALU.mult)
                    done(m)
                    for e in range(E):
                        for h in range(2):
                            if e:
                                dve.wait_ge(one_used, 2 * e + h - 1)
                            shape = (HT, B, HT)
                            col = h * P + e * B
                            dve.tensor_tensor(onelo[h][:], lo[:, col:col + B].unsqueeze(2).to_broadcast(shape),
                                              const(C_IOTA, HT)[0:HT].unsqueeze(1).to_broadcast(shape),
                                              ALU.is_equal).then_inc(one_ready, 1)
                    dve.wait_ge(one_used, 2 * E)
                    done(dve.tensor_copy(tab[:], psQ[0:HT, 0:10 * E].rearrange("p (e v t) -> p e v t", e=E, v=2)))
                    done(dve.tensor_tensor(tok[:], tab[:, :, 0, :], tab[:, :, 1, :], ALU.add))
                    done(dve.tensor_scalar(row[:], tok[:], -1.0, 0.0, ALU.add, ALU.max))
                    done(dve.tensor_scalar(skip[:], tok[:], 0.5, float(2 * N), ALU.is_lt, ALU.mult))
                    done(dve.tensor_tensor(skip[:], skip[:], row[:], ALU.add))
                    dve.tensor_copy(gather_rows[:].rearrange("p (e t) -> p e t", e=E), row[:])
                    dve.tensor_copy(scatter_rows[:].rearrange("p (e t) -> p e t", e=E), skip[:]).then_inc(tabled, 1)

        with ExitStack() as c:
            raw_g, raw_u, raw_d = ([sb(c, f"raw_{m}{i}", [P, D]) for i in range(2)] for m in "gud")
            g_hi, u_hi, d_hi = ([sb(c, f"{m}_hi{i}", [P, D], F32R) for i in range(2)] for m in "gud")
            g_lo, u_lo, d_lo = ([sb(c, f"{m}_lo{i}", [P, D], F32R) for i in range(2)] for m in "gud")
            xg = sb(c, "xg", [HT, SLOT_TILES, XW])
            x_hi, x_lo = (sb(c, n, [P, KD, CAP], F32R) for n in ("ex_hi", "ex_lo"))
            act_g, h, h_hi, h_lo = ([sb(c, f"{n}{i}", [P, CAP], dt) for i in range(2)]
                                    for n, dt in (("act_g", F32), ("hid", F32), ("hid_hi", F32R), ("hid_lo", F32R)))
            wcol = sb(c, "wcol", [HT, SLOT_TILES])
            y, cur = (sb(c, n, [HT, SLOT_TILES, D]) for n in ("ex_y", "ex_cur"))
            gidx, sidx = (sb(c, n, [HT, SLOT_TILES], U32) for n in ("gidx", "sidx"))
            psG, psU, psT = (psum(c, "e_" + n) for n in ("psG", "psU", "psT"))
            psY = [psum(c, f"e_psY{t}") for t in range(SLOT_TILES)]
            load = {m: [sem(f"load_{m}{i}") for i in range(2)] for m in "gud"}
            names = ("gate", "gu_hi", "gu_lo", "d_hi", "d_lo", "up", "silu", "mul", "h_hi", "h_lo", "down", "y_full", "y_out",
                     "x_up", "x_hi", "x_lo", "wcol", "gidx", "xg", "cur", "added", "scat", "sidx")
            S = {n: sem("e_" + n) for n in names}
            CH = CAP // 2
            halves = (slice(0, CH), slice(CH, CAP))
            psx = (psT, psG)

            with nc.Block() as block:
                @block.sync
                def _(sp):
                    def sl(view, e, dims):
                        return view[e] if isinstance(e, int) else view[bass.ds(e, 1)].rearrange(dims)

                    def fetch(e, f, i, first):
                        n = FT * e + f
                        cols = slice(f * P, f * P + P) if isinstance(f, int) else bass.ds(f * P, P)
                        for k, (m, src, dst) in enumerate((("g", w_g, raw_g), ("u", w_u, raw_u))):
                            if not first:
                                hold(sp, S["gate"], S["gu_lo"], 2 * n - 3 + k)
                            v = src[e].rearrange("(k p) f -> p k f", p=P)[:, :, cols] if isinstance(e, int) else \
                                src[bass.ds(e, 1), :, cols].rearrange("o (k p) f -> (o p) k f", p=P)
                            sp.dma_start(dst[i][:].rearrange("p (k f) -> p k f", k=KD), v).then_inc(load[m][i], 16)
                        if not first:
                            hold(sp, S["gate"], S["d_lo"], n - 1)
                        v = w_d[e, cols, :] if isinstance(e, int) else w_d[bass.ds(e, 1), cols, :].rearrange("o p d -> (o p) d")
                        sp.dma_start(raw_d[i][:], v).then_inc(load["d"][i], 16)

                    fetch(0, 0, 0, True)
                    fetch(0, 1, 1, True)
                    with sp.Fori(1, FT // 2) as q:
                        for i in range(2):
                            fetch(0, 2 * q + i, i, False)
                    with sp.Fori(1, E) as e:
                        with sp.Fori(0, FT // 2) as q:
                            for i in range(2):
                                fetch(e, 2 * q + i, i, False)
                    sp.wait_ge(S["scat"], 16 * SLOT_TILES * E)

                @block.gpsimd
                def _(pool):
                    def fetch_rows():
                        for t in range(SLOT_TILES):
                            pool.indirect_dma_start(xg[:, t, :], None, rows_w, bass.IndirectOffsetOnAxis(ap=gidx[:, t:t + 1], axis=0),
                                                    bounds_check=N - 1, oob_is_err=False).then_inc(S["xg"], 16)

                    G = 16 * SLOT_TILES
                    pool.tensor_copy(gidx[:], gather_rows[:, 0:SLOT_TILES]).then_inc(S["gidx"], 1)
                    pool.wait_ge(S["gidx"], 1)
                    fetch_rows()

                    def expert(e, last):
                        pool.tensor_copy(sidx[:], scatter_rows[:, bass.ds(SLOT_TILES * e, SLOT_TILES)]).then_inc(S["sidx"], 1)
                        for t in range(SLOT_TILES):
                            pool.indirect_dma_start(cur[:, t, :], None, out, bass.IndirectOffsetOnAxis(ap=gidx[:, t:t + 1], axis=0),
                                                    bounds_check=N - 1, oob_is_err=False).then_inc(S["cur"], 16)
                        pool.wait_ge(S["cur"], G * e + G)
                        if not last:
                            hold(pool, S["gate"], S["xg"], G * e + G)
                            pool.tensor_copy(gidx[:], gather_rows[:, bass.ds(SLOT_TILES * e + SLOT_TILES, SLOT_TILES)]).then_inc(S["gidx"], 1)
                            hold(pool, S["gate"], S["gidx"], e + 2)
                            hold(pool, S["gate"], S["x_up"], SLOT_TILES * e + SLOT_TILES)
                            hold(pool, S["gate"], S["wcol"], e + 1)
                            fetch_rows()
                        pool.wait_ge(S["y_out"], SLOT_TILES * e + SLOT_TILES)
                        pool.tensor_tensor(y[:], y[:], cur[:], ALU.add).then_inc(S["added"], 1)
                        hold(pool, S["gate"], S["added"], e + 1)
                        hold(pool, S["gate"], S["sidx"], e + 1)
                        for t in range(SLOT_TILES):
                            pool.indirect_dma_start(out, bass.IndirectOffsetOnAxis(ap=sidx[:, t:t + 1], axis=0), y[:, t, :], None,
                                                    bounds_check=N - 1, oob_is_err=False).then_inc(S["scat"], 16)
                        hold(pool, S["gate"], S["scat"], G * e + G)

                    with pool.Fori(0, E - 1) as e:
                        expert(e, False)
                    expert(E - 1, True)

                @block.tensor
                def _(pe):
                    def turn(e, first):
                        pe.wait_ge(S["xg"], 16 * SLOT_TILES * e + 16 * SLOT_TILES)
                        for t in range(SLOT_TILES):
                            if t >= 2:
                                pe.wait_ge(S["x_lo"], SLOT_TILES * e + t - 1)
                            elif t == 1 and not first:
                                pe.wait_ge(S["silu"], 2 * FT * e)
                            for k in range(KD):
                                m = pe.transpose(psx[t % 2][:, k * HT:(k + 1) * HT], xg[:, t, k * P:(k + 1) * P], ident[0:HT, 0:HT])
                            m.then_inc(S["x_up"], 1)

                    def unit(n, i, wh, wl, bank, s):
                        for k in range(KD):
                            cols = slice(k * P, (k + 1) * P)
                            m = mm3(pe, bank[:, 0:CH], (wh[:, cols], wl[:, cols]), (x_hi[:, k, halves[s]], x_lo[:, k, halves[s]]),
                                    k == 0, k == KD - 1)
                        m.then_inc(S["up"], 1)

                    def up(n, i, s, start=False):
                        if s == 0:
                            pe.wait_ge(S["gu_lo"], 2 * n + 1)
                        if not (start and s == 0):
                            pe.wait_ge(S["silu"], 2 * n + s)
                        unit(n, i, g_hi[i], g_lo[i], psG, s)
                        if s == 0:
                            pe.wait_ge(S["gu_lo"], 2 * n + 2)
                        if not (start and s == 0):
                            pe.wait_ge(S["mul"], 2 * n + s)
                        unit(n, i, u_hi[i], u_lo[i], psU, s)

                    def down(n, i, first, last, lo, hi, e=None):
                        if lo == 0:
                            pe.wait_ge(S["d_lo"], n + 1)
                            pe.wait_ge(S["h_lo"], 2 * n + 2)
                        for t in range(lo, hi):
                            if first and e is not None:
                                pe.wait_ge(S["y_out"], SLOT_TILES * e)
                            cols = slice(t * HT, (t + 1) * HT)
                            m = mm3(pe, psY[t][0:HT, :], (h_hi[i][:, cols], h_lo[i][:, cols]), (d_hi[i][:], d_lo[i][:]), first, last)
                            if last:
                                m.then_inc(S["y_full"], 1)
                        if hi == SLOT_TILES and not last:
                            m.then_inc(S["down"], 1)

                    turn(0, True)

                    def expert(e, start, last):
                        n = FT * e
                        pe.wait_ge(S["x_lo"], SLOT_TILES * e + SLOT_TILES)
                        up(n, 0, 0, start)
                        up(n, 0, 1)
                        ee = None if start else e
                        up(n + 1, 1, 0)
                        down(n, 0, True, False, 0, 2, ee)
                        up(n + 1, 1, 1)
                        down(n, 0, True, False, 2, SLOT_TILES)
                        up(n + 2, 0, 0)
                        down(n + 1, 1, False, False, 0, 2)
                        up(n + 2, 0, 1)
                        down(n + 1, 1, False, False, 2, SLOT_TILES)
                        with pe.Fori(1, FT // 2 - 1) as q:
                            for i in (1, 0):
                                m = n + 2 * q + 2 - i
                                up(m, i, 0)
                                down(m - 1, 1 - i, False, False, 0, 2)
                                up(m, i, 1)
                                down(m - 1, 1 - i, False, False, 2, SLOT_TILES)
                        m = n + FT - 1
                        up(m, 1, 0)
                        down(m - 1, 0, False, False, 0, 2)
                        up(m, 1, 1)
                        down(m - 1, 0, False, False, 2, SLOT_TILES)
                        if not last:
                            turn(e + 1, False)
                        down(m, 1, False, True, 0, SLOT_TILES)

                    expert(0, True, False)
                    with pe.Fori(1, E - 1) as e:
                        expert(e, False, False)
                    expert(E - 1, False, True)

                @block.scalar
                def _(act):
                    def high(m, i, value, raw, hi, count):
                        act.wait_ge(load[m][i], value)
                        act.activation(hi[i][:], raw[i][:], ACT.Copy).then_inc(S[count], 1)

                    def step(n, half, i, next_=True):
                        def silu(s):
                            act.wait_ge(S["up"], 4 * n + 2 * s + 1)
                            act.activation(act_g[i][:, halves[s]], psG[:, 0:CH], ACT.Silu).then_inc(S["silu"], 1)

                        def split_h(s):
                            act.wait_ge(S["mul"], 2 * n + s + 1)
                            act.activation(h_hi[i][:, halves[s]], h[i][:, halves[s]], ACT.Copy).then_inc(S["h_hi"], 1)

                        v = 16 * (half + 1 + i)
                        silu(0)
                        if next_:
                            high("g", 1 - i, v, raw_g, g_hi, "gu_hi")
                        split_h(0)
                        silu(1)
                        if next_:
                            high("u", 1 - i, v, raw_u, u_hi, "gu_hi")
                        split_h(1)
                        high("d", i, 16 * (half + 1), raw_d, d_hi, "d_hi")

                    def split_x(e):
                        for t in range(SLOT_TILES):
                            act.wait_ge(S["x_up"], SLOT_TILES * e + t + 1)
                            act.activation(x_hi[:, :, t * HT:(t + 1) * HT],
                                           psx[t % 2][:, 0:KD * HT].rearrange("p (k t) -> p k t", k=KD), ACT.Copy).then_inc(S["x_hi"], 1)

                    def weights(e):
                        act.wait_ge(S["xg"], 16 * SLOT_TILES * e + 16 * SLOT_TILES)
                        col = xg[:, :, D:D + 1] if isinstance(e, int) and e == 0 else xg[:, :, bass.ds(D + e, 1)]
                        act.activation(wcol[:].unsqueeze(2), col, ACT.Copy).then_inc(S["wcol"], 1)

                    def expert(e, last):
                        n, half = FT * e, FT // 2 * e
                        step(n, half, 0)
                        with act.Fori(0, FT // 2 - 1) as q:
                            step(n + 2 * q + 1, half + q, 1)
                            step(n + 2 * q + 2, half + q + 1, 0)
                        step(n + FT - 1, half + FT // 2 - 1, 1, not last)
                        if not last:
                            split_x(e + 1)
                        act.wait_ge(S["wcol"], e + 1)
                        if not (isinstance(e, int) and e == 0):
                            act.wait_ge(S["scat"], 16 * SLOT_TILES * e)
                        for t in range(SLOT_TILES):
                            act.wait_ge(S["y_full"], SLOT_TILES * e + t + 1)
                            act.activation(y[:, t, :], psY[t][0:HT, :], ACT.Copy, scale=wcol[:, t:t + 1]).then_inc(S["y_out"], 1)
                        if not last:
                            act.wait_ge(S["y_out"], SLOT_TILES * e + SLOT_TILES)
                            weights(e + 1)

                    high("g", 0, 16, raw_g, g_hi, "gu_hi")
                    high("u", 0, 16, raw_u, u_hi, "gu_hi")
                    split_x(0)
                    weights(0)
                    expert(0, False)
                    with act.Fori(1, E - 1) as e:
                        expert(e, False)
                    expert(E - 1, True)

                @block.vector
                def _(dve):
                    def low(i, value, raw, hi, lo, counted, count):
                        dve.wait_ge(S[counted], value)
                        dve.tensor_tensor(lo[i][:], raw[i][:], hi[i][:].bitcast(F32), ALU.subtract).then_inc(S[count], 1)

                    def step(n, i, next_=True):
                        def multiply(s):
                            dve.wait_ge(S["silu"], 2 * n + s + 1)
                            dve.wait_ge(S["up"], 4 * n + 2 * s + 2)
                            dve.tensor_tensor(h[i][:, halves[s]], psU[:, 0:CH], act_g[i][:, halves[s]], ALU.mult).then_inc(S["mul"], 1)

                        def split_h(s):
                            dve.wait_ge(S["h_hi"], 2 * n + s + 1)
                            dve.tensor_tensor(h_lo[i][:, halves[s]], h[i][:, halves[s]], h_hi[i][:, halves[s]].bitcast(F32),
                                              ALU.subtract).then_inc(S["h_lo"], 1)

                        multiply(0)
                        if next_:
                            low(1 - i, 2 * n + 3, raw_g, g_hi, g_lo, "gu_hi", "gu_lo")
                        split_h(0)
                        multiply(1)
                        if next_:
                            low(1 - i, 2 * n + 4, raw_u, u_hi, u_lo, "gu_hi", "gu_lo")
                        split_h(1)
                        low(i, n + 1, raw_d, d_hi, d_lo, "d_hi", "d_lo")

                    def split_x(e):
                        for t in range(SLOT_TILES):
                            cols = slice(t * HT, (t + 1) * HT)
                            dve.wait_ge(S["x_hi"], SLOT_TILES * e + t + 1)
                            dve.tensor_tensor(x_lo[:, :, cols], psx[t % 2][:, 0:KD * HT].rearrange("p (k t) -> p k t", k=KD),
                                              x_hi[:, :, cols].bitcast(F32), ALU.subtract).then_inc(S["x_lo"], 1)

                    def expert(e, last):
                        n = FT * e
                        step(n, 0)
                        with dve.Fori(0, FT // 2 - 1) as q:
                            step(n + 2 * q + 1, 1)
                            step(n + 2 * q + 2, 0)
                        step(n + FT - 1, 1, not last)
                        if not last:
                            split_x(e + 1)

                    low(0, 1, raw_g, g_hi, g_lo, "gu_hi", "gu_lo")
                    low(0, 2, raw_u, u_hi, u_lo, "gu_hi", "gu_lo")
                    split_x(0)
                    with dve.Fori(0, E - 1) as e:
                        expert(e, False)
                    expert(E - 1, True)


def decoder_layer(nc, x, ctx, cmask, w_in, b_in, w_out, b_out, w_q, w_k, w_v, w_o, router_w, w_g, w_u, w_d, cst, out):
    x1 = nc.dram_tensor("after_self_attention", [N, D], F32, kind="Internal").ap()
    rows_w = nc.dram_tensor("expert_rows", [N, XW], F32, kind="Internal").ap()
    flat = out.rearrange("b t d -> (b t) d")
    self_attention(nc, x, w_in, b_in, w_out, b_out, cst, x1)
    cross_attention(nc, x1, ctx, cmask, w_q, w_k, w_v, w_o, cst, flat)
    experts(nc, flat, router_w, w_g, w_u, w_d, cst, rows_w)


INPUTS = ["x", "ctx_768", "mask_BxS2_bf1", "L0_attn_W_in", "L0_attn_b_in", "L0_attn_W_out", "L0_attn_b_out",
          "L0_xattn_Wq", "L0_xattn_Wk", "L0_xattn_Wv", "L0_xattn_Wo",
          "L0_ffn_router_w", "L0_ffn_wg", "L0_ffn_wu", "L0_ffn_wd"]


def kernel(**inputs):
    import concourse.bacc as bacc
    from concourse.bass_utils import run_bass_kernel_spmd

    nc = bacc.Bacc("TRN2", target_bir_lowering=False, num_devices=1)
    arrays = {name: np.ascontiguousarray(inputs[name]) for name in INPUTS}
    arrays["mask_BxS2_bf1"] = arrays["mask_BxS2_bf1"].view(np.uint8)
    arrays["shape_constants"] = all_constants()
    arrays = {f"in_{name}": a for name, a in arrays.items()}
    args = [nc.dram_tensor(name, a.shape, mybir.dt.from_np(a.dtype), kind="ExternalInput").ap() for name, a in arrays.items()]
    args.append(nc.dram_tensor("out_0", [B, T, D], F32, kind="ExternalOutput").ap())
    decoder_layer(nc, *args)
    return run_bass_kernel_spmd(nc, [arrays], core_ids=[0]).results[0]["out_0"]
```
